# Optimizing a Trainium2 kernel written in Bass

```python
import numpy as np
import jax
import jax.numpy as jnp

def _softmax(x, axis=-1):
    return jax.nn.softmax(x, axis=axis)

def _gelu(x):
    return jax.nn.gelu(x, approximate=True)

def _silu(x):
    return jax.nn.silu(x)

def _sigmoid(x):
    return jax.nn.sigmoid(x)

def _layernorm(x, axis=-1, eps=1e-05):
    m = jnp.mean(x, axis=axis, keepdims=True)
    v = jnp.var(x, axis=axis, keepdims=True)
    return (x - m) / jnp.sqrt(v + eps)

def _scatter_add(tgt, idx, src, axis=0):
    return tgt.at[idx].add(src)

def _segment_sum(src, seg, n):
    return jax.ops.segment_sum(src, seg, n)
kernel_name = 'mk_conv_seq_d2_conv_nchw128_r2_251faa'

def setup_inputs(seed: int=0):
    np.random.seed(seed)
    _w = jnp.asarray

    def _rec_inputs():
        import jax
        import jax.numpy as jnp
        _gk = jax.random.key(seed)
        x = -0.0003929 + 0.9999 * jax.random.normal(jax.random.fold_in(_gk, 1), (8, 64, 64, 64), jnp.float32)
        return x
    x = _rec_inputs()

    def _L0_conv_setup():
        import jax, jax.numpy as jnp
        import numpy as np
        from jax import lax
        B, C, H, W = (8, 64, 64, 64)
        KW = 9
        PW = (KW - 1) // 2

        def _make_kernel(key):
            std = float(np.sqrt(2.0 / (C * KW * C)))
            return jax.random.normal(key, (KW, C, C), dtype=jnp.float32) * std

        def _row_conv(y, K):
            return lax.conv_general_dilated(y, K, window_strides=(1,), padding=[(PW, PW)], dimension_numbers=('NWC', 'WIO', 'NWC'))

        def _dir_scan(x, K, reverse):
            if reverse:
                x = x[:, ::-1]

            def step(prev, cur):
                new = cur + jax.nn.relu(_row_conv(prev, K))
                return (new, new)
            first = x[:, 0]
            _, rest = lax.scan(step, first, jnp.moveaxis(x[:, 1:], 1, 0))
            out = jnp.concatenate([first[:, None], jnp.moveaxis(rest, 0, 1)], axis=1)
            if reverse:
                out = out[:, ::-1]
            return out
        key = jax.random.key(seed)
        kx, k1, k2, k3, k4 = jax.random.split(key, 5)
        x = jax.random.normal(kx, (B, C, H, W), dtype=jnp.float32)
        return {'x': x, 'k_td': _make_kernel(k1), 'k_dt': _make_kernel(k2), 'k_lr': _make_kernel(k3), 'k_rl': _make_kernel(k4)}
    _L0_conv_all = _L0_conv_setup()
    _L0_conv_in = {k: v for k, v in _L0_conv_all.items() if k in ('k_td', 'k_dt', 'k_lr', 'k_rl')}
    del _L0_conv_all

    def _L1_conv_setup():
        import jax, jax.numpy as jnp
        import numpy as np
        from jax import lax
        B, C, H, W, K = (32, 64, 56, 56, 5)
        CR = C // 4
        CE = 4 * C
        EPS = 1e-06

        def _ln(v, w, b, axis):
            u = v.mean(axis, keepdims=True)
            s2 = jnp.square(v - u).mean(axis, keepdims=True)
            return (v - u) * lax.rsqrt(s2 + EPS) * w + b
        key = jax.random.key(seed)
        ks = jax.random.split(key, 8)
        s = lambda fan: 1.0 / np.sqrt(fan)
        return {'x': jax.random.normal(ks[0], (B, C, H, W), jnp.float32), 'w_fc1': jax.random.normal(ks[1], (CR, C), jnp.float32) * s(C), 'ln1_w': jnp.ones((CR,), jnp.float32), 'ln1_b': jnp.zeros((CR,), jnp.float32), 'w_fc2': jax.random.normal(ks[2], (C * K * K, CR), jnp.float32) * s(CR), 'ln2_w': jnp.ones((C,), jnp.float32), 'ln2_b': jnp.zeros((C,), jnp.float32), 'w_expand': jax.random.normal(ks[3], (CE, C), jnp.float32) * s(C), 'w_shrink': jax.random.normal(ks[4], (C, CE), jnp.float32) * s(CE), 'grn_gamma': jax.random.normal(ks[5], (CE,), jnp.float32) * 0.1, 'grn_beta': jax.random.normal(ks[6], (CE,), jnp.float32) * 0.1}
    _L1_conv_all = _L1_conv_setup()
    _L1_conv_in = {k: v for k, v in _L1_conv_all.items() if k in ('w_fc1', 'ln1_w', 'ln1_b', 'w_fc2', 'ln2_w', 'ln2_b', 'w_expand', 'w_shrink', 'grn_gamma', 'grn_beta')}
    del _L1_conv_all
    return {'x': x, 'L0_conv_k_td': _L0_conv_in['k_td'], 'L0_conv_k_dt': _L0_conv_in['k_dt'], 'L0_conv_k_lr': _L0_conv_in['k_lr'], 'L0_conv_k_rl': _L0_conv_in['k_rl'], 'L1_conv_w_fc1': _L1_conv_in['w_fc1'], 'L1_conv_ln1_w': _L1_conv_in['ln1_w'], 'L1_conv_ln1_b': _L1_conv_in['ln1_b'], 'L1_conv_w_fc2': _L1_conv_in['w_fc2'], 'L1_conv_ln2_w': _L1_conv_in['ln2_w'], 'L1_conv_ln2_b': _L1_conv_in['ln2_b'], 'L1_conv_w_expand': _L1_conv_in['w_expand'], 'L1_conv_w_shrink': _L1_conv_in['w_shrink'], 'L1_conv_grn_gamma': _L1_conv_in['grn_gamma'], 'L1_conv_grn_beta': _L1_conv_in['grn_beta']}

def reference(x, L0_conv_k_td, L0_conv_k_dt, L0_conv_k_lr, L0_conv_k_rl, L1_conv_w_fc1, L1_conv_ln1_w, L1_conv_ln1_b, L1_conv_w_fc2, L1_conv_ln2_w, L1_conv_ln2_b, L1_conv_w_expand, L1_conv_w_shrink, L1_conv_grn_gamma, L1_conv_grn_beta):
    import jax
    import jax.numpy as jnp

    def _L0_conv_ref(x, k_td, k_dt, k_lr, k_rl):
        import jax, jax.numpy as jnp
        import numpy as np
        from jax import lax
        B, C, H, W = (8, 64, 64, 64)
        KW = 9
        PW = (KW - 1) // 2

        def _make_kernel(key):
            std = float(np.sqrt(2.0 / (C * KW * C)))
            return jax.random.normal(key, (KW, C, C), dtype=jnp.float32) * std

        def _row_conv(y, K):
            return lax.conv_general_dilated(y, K, window_strides=(1,), padding=[(PW, PW)], dimension_numbers=('NWC', 'WIO', 'NWC'))

        def _dir_scan(x, K, reverse):
            if reverse:
                x = x[:, ::-1]

            def step(prev, cur):
                new = cur + jax.nn.relu(_row_conv(prev, K))
                return (new, new)
            first = x[:, 0]
            _, rest = lax.scan(step, first, jnp.moveaxis(x[:, 1:], 1, 0))
            out = jnp.concatenate([first[:, None], jnp.moveaxis(rest, 0, 1)], axis=1)
            if reverse:
                out = out[:, ::-1]
            return out
        y = jnp.transpose(x, (0, 2, 3, 1))
        y = _dir_scan(y, k_td, reverse=False)
        y = _dir_scan(y, k_dt, reverse=True)
        yt = jnp.swapaxes(y, 1, 2)
        yt = _dir_scan(yt, k_lr, reverse=False)
        yt = _dir_scan(yt, k_rl, reverse=True)
        y = jnp.swapaxes(yt, 1, 2)
        return jnp.transpose(y, (0, 3, 1, 2))

    def _L1_conv_ref(x, w_fc1, ln1_w, ln1_b, w_fc2, ln2_w, ln2_b, w_expand, w_shrink, grn_gamma, grn_beta):
        import jax, jax.numpy as jnp
        import numpy as np
        from jax import lax
        B, C, H, W, K = (32, 64, 56, 56, 5)
        CR = C // 4
        CE = 4 * C
        EPS = 1e-06

        def _ln(v, w, b, axis):
            u = v.mean(axis, keepdims=True)
            s2 = jnp.square(v - u).mean(axis, keepdims=True)
            return (v - u) * lax.rsqrt(s2 + EPS) * w + b
        b, c, h, w = x.shape
        pooled = x.mean((2, 3))
        hdn = pooled @ w_fc1.T
        hdn = _ln(hdn, ln1_w, ln1_b, axis=-1)
        dyn = hdn @ w_fc2.T
        dyn_w = dyn.reshape(b * c, 1, K, K)
        pad = K // 2
        out = lax.conv_general_dilated(x.reshape(1, b * c, h, w), dyn_w, window_strides=(1, 1), padding=[(pad, pad), (pad, pad)], dimension_numbers=('NCHW', 'OIHW', 'NCHW'), feature_group_count=b * c).reshape(b, c, h, w)
        u = out.mean(1, keepdims=True)
        s2 = jnp.square(out - u).mean(1, keepdims=True)
        out = (out - u) * lax.rsqrt(s2 + EPS)
        out = ln2_w[None, :, None, None] * out + ln2_b[None, :, None, None]
        out = jnp.einsum('bchw,oc->bohw', out, w_expand)
        out = jax.nn.gelu(out, approximate=False)
        gx = jnp.sqrt(jnp.sum(jnp.square(out), axis=(2, 3), keepdims=True))
        nx = gx / (gx.mean(1, keepdims=True) + EPS)
        g = grn_gamma[None, :, None, None]
        bt = grn_beta[None, :, None, None]
        out = g * (out * nx) + bt + out
        out = jnp.einsum('bohw,co->bchw', out, w_shrink)
        return out + x

    def _gn(v, G=32, eps=1e-05):
        B_, C_, H_, W_ = v.shape
        g = v.reshape(B_, G, C_ // G, H_, W_)
        m = jnp.mean(g, axis=(2, 3, 4), keepdims=True)
        s = jnp.var(g, axis=(2, 3, 4), keepdims=True)
        return ((g - m) / jnp.sqrt(s + eps)).reshape(v.shape)

    def _ln_c(v, eps=1e-06):
        m = jnp.mean(v, axis=1, keepdims=True)
        s = jnp.var(v, axis=1, keepdims=True)
        return (v - m) / jnp.sqrt(s + eps)

    def _ln_t(v, eps=1e-05):
        m = jnp.mean(v, axis=-1, keepdims=True)
        s = jnp.var(v, axis=-1, keepdims=True)
        return (v - m) / jnp.sqrt(s + eps)

    def _to_tokens(v):
        B_, C_, H_, W_ = v.shape
        return v.reshape(B_, C_, H_ * W_).transpose(0, 2, 1)

    def _from_tokens(t, like):
        B_, C_, H_, W_ = like.shape
        return t.transpose(0, 2, 1).reshape(B_, C_, H_, W_)
    x = _L0_conv_ref(x, L0_conv_k_td, L0_conv_k_dt, L0_conv_k_lr, L0_conv_k_rl)
    x = _L1_conv_ref(x, L1_conv_w_fc1, L1_conv_ln1_w, L1_conv_ln1_b, L1_conv_w_fc2, L1_conv_ln2_w, L1_conv_ln2_b, L1_conv_w_expand, L1_conv_w_shrink, L1_conv_grn_gamma, L1_conv_grn_beta)
    return x

_drawn_inputs = setup_inputs


def setup_inputs(seed=0):
    import zlib

    import numpy as np

    out = dict(_drawn_inputs(seed))
    spreads = {'L1_conv_ln1_w': (1.0, 0.2),
     'L1_conv_ln1_b': (0.0, 0.1),
     'L1_conv_ln2_w': (1.0, 0.2),
     'L1_conv_ln2_b': (0.0, 0.1)}
    factors = {}
    for name, (base, spread) in spreads.items():
        noise = np.random.default_rng([zlib.crc32(name.encode()), seed]).standard_normal(out[name].shape)
        drawn = base * np.exp(spread * noise) if base else spread * noise
        out[name] = jnp.asarray(drawn.astype(out[name].dtype))
    for name, factor in factors.items():
        out[name] = (out[name] * factor).astype(out[name].dtype)
    return out
```

```python
from contextlib import ExitStack

import concourse.bass as bass
from concourse import mybir

F32 = mybir.dt.float32
F32R = mybir.dt.float32r
ALU = mybir.AluOpType
ACT = mybir.ActivationFunctionType
AX = mybir.AxisListType

P = 128
B, C, H, W = 8, 64, 64, 64
TAPS = 9
REACH = 2
OFFSETS = 2 * REACH + 1
WP, HP = W // 2, H // 2
PADDED = WP + 2 * REACH
LINE = B * WP
ROWS_A_LOAD = 8
LOADS = H // ROWS_A_LOAD
BG = B // 2

K = 5
KD = 3
CR, CE = C // 4, 4 * C
HALVES = CE // P
EPS = 1e-6
LN1 = 8
PIX = W * HP
CHUNKS = 4
CW = W // CHUNKS
COLS = PIX // CHUNKS
STAT_COLS = 128
STATS = PIX // STAT_COLS
STAT_ROWS = 2 * STATS
XW, XJ = W + K - 1, HP + 2


def build(nc, x, k_td, k_dt, k_lr, k_rl, fc1, ln1_w, ln1_b, fc2, ln2_w, ln2_b,
          expand, shrink, gamma, beta, out):
    with ExitStack() as ctx:
        ctx.enter_context(nc.allow_non_contiguous_dma(reason="small parameters and rows of images"))
        bank = [ctx.enter_context(nc.psum_tensor(f"bank{i}", [P, 512], F32)) for i in range(8)]

        def sb(name, shape, dt=F32):
            return ctx.enter_context(nc.sbuf_tensor(name, shape, dt))

        kept = dict(
            by_h=sb("by_h", [P, B, W, HP]),
            ident=sb("ident", [P, P]),
            centre=sb("centre", [P, C]),
            pick=sb("pick", [P, 2 * STAT_ROWS - 2]),
            mean_ce=sb("mean_ce", [P, P]),
            fc1_t=sb("fc1_t", [P, CR]),
            ln1_wb=sb("ln1_wb", [LN1, 2, CR]),
            expand_t=sb("expand_t", [P, HALVES, P]),
            expand_bias=sb("expand_bias", [P, HALVES]),
            shrink_t=sb("shrink_t", [P, HALVES, 2, C]),
            gamma=sb("gamma", [P, HALVES]),
            out_bias=sb("out_bias", [P, 1]),
        )
        at = -(-nc.sbuf_base // 32) * 32
        full_bytes = 4 * KD * K * P
        sb("slab", [P, KD * K * P + STAT_ROWS * C])
        kept["fc2_t"] = nc.alloc_sbuf_tensor_at("fc2_t", [CR, K * K, P], F32, offset=at)
        kept["dyn_all"] = nc.alloc_sbuf_tensor_at("dyn_all", [P, KD * K, 2, C], F32, offset=at)
        kept["spread"] = nc.alloc_sbuf_tensor_at("spread", [STAT_ROWS, STAT_ROWS, C], F32R,
                                                 offset=at + full_bytes)
        scans(nc, bank, kept, x, (k_td, k_dt, k_lr, k_rl), fc1, ln1_w, ln1_b, fc2, ln2_w, ln2_b,
              expand, shrink, gamma, beta)
        block_two(nc, bank, kept, out)


def scans(nc, bank, kept, x, kernels, fc1, ln1_w, ln1_b, fc2, ln2_w, ln2_b,
          expand, shrink, gamma, beta):
    by_h, ident = kept["by_h"], kept["ident"]
    main_ps, low_ps, prep_ps = bank[0:2], bank[2:4], bank[4:8]
    with ExitStack() as ctx:
        def sb(name, shape, dt=F32):
            return ctx.enter_context(nc.sbuf_tensor(name, shape, dt))

        def sem(name):
            return ctx.enter_context(nc.semaphore(name))

        by_w = sb("by_w", [P, B, H, WP])
        stage = sb("stage", [P, 2, BG, ROWS_A_LOAD, W])
        taps = sb("taps", [P, OFFSETS, 2, C])
        taps_hi = sb("taps_hi", [P, 4, OFFSETS, P], F32R)
        taps_lo = sb("taps_lo", [P, 4, OFFSETS, P], F32R)
        line_hi = sb("line_hi", [P, 2, B, PADDED], F32R)
        line_lo = sb("line_lo", [P, 2, B, PADDED], F32R)
        main_sb = sb("main_sb", [P, 2, LINE])
        both = sb("both", [P, LINE])
        rest = sb("rest", [P, LINE])
        fc1_in = sb("fc1_in", [CR, 2, C])
        fc2_in = sb("fc2_in", [P, K * K, CR])
        expand_in = sb("expand_in", [P, HALVES, 2, C])
        shrink_in = sb("shrink_in", [C, CE])
        ln2 = sb("ln2", [P, 2])
        beta_in = sb("beta_in", [P, HALVES])
        later = by_h[:, 0, :, :].rearrange("p w j -> p (w j)")[:, 0:3 * OFFSETS * P]
        raw = [taps[:, :, :, :]] + [
            later.rearrange("p (s d o c) -> p s d o c", s=3, d=OFFSETS, o=2)[:, n, :, :, :] for n in range(3)]

        x_loaded = [sem(f"x_loaded{i}") for i in range(2)]
        x_spread = sem("x_spread")
        taps_zero = sem("taps_zero")
        taps_loaded = [sem(f"taps_loaded{i}") for i in range(4)]
        taps_high = sem("taps_high")
        taps_ready = sem("taps_ready")
        line_zero = sem("line_zero")
        main_done = sem("main_done")
        low_done = sem("low_done")
        high_ready = sem("high_ready")
        low_ready = sem("low_ready")
        main_copied = sem("main_copied")
        rest_ready = sem("rest_ready")
        both_ready = sem("both_ready")
        line_done = sem("line_done")
        turned = sem("turned")
        params = sem("params")
        ident_zero = sem("ident_zero")
        ident_ready = sem("ident_ready")
        prep_mm = sem("prep_mm")
        prep_ev = sem("prep_ev")
        consts = sem("consts")

        N_PARAMS = 15

        counts = [H, H - 1, W, W - 1]
        first = [sum(counts[:s]) for s in range(4)]

        def line(s, r):
            image = by_w if s < 2 else by_h
            if isinstance(r, int):
                return image[:, :, r, :]
            return image[:, :, bass.ds(r, 1), :].rearrange("p b a i -> p b (a i)")

        def run(engine, s, step):
            n0, count = first[s], counts[s]
            row = (lambda k: k) if s % 2 == 0 else (lambda k: k * -1 + (count - 1))
            with engine.Fori(0, count // 2) as i:
                for u in range(2):
                    step(n0 + u + 2 * i, row(2 * i + u), (n0 + u) % 2)
            if count % 2:
                k = count - 1
                step(n0 + k, row(k), (n0 + k) % 2)

        block = ctx.enter_context(nc.Block())

        @block.sync
        def _(sp):
            def load(n):
                for g in range(2):
                    sp.dma_start(
                        stage[C * g:C * g + C, n % 2, :, :, :].rearrange("c b h w -> c b (h w)"),
                        x[BG * g:BG * g + BG, :, ROWS_A_LOAD * n:ROWS_A_LOAD * (n + 1), :]
                        .rearrange("b c h w -> c b (h w)")).then_inc(x_loaded[n % 2], 16)

            def load_taps(s):
                k = kernels[s].rearrange("t i o -> i t o")
                for pi in range(2):
                    for po in range(2):
                        lo = pi - po
                        d0 = 1 if lo < 0 else 0
                        n = OFFSETS - abs(lo)
                        t0 = lo + 2 * d0
                        sp.dma_start(raw[s][C * pi:C * pi + C, d0:d0 + n, po, :],
                                     k[:, t0:t0 + 2 * n - 1:2, :]).then_inc(taps_loaded[s], 16)

            load(0)
            sp.wait_ge(taps_zero, 1)
            load_taps(0)
            load(1)
            for s in range(1, 4):
                load_taps(s)
            sp.dma_start(fc1_in[:, 0, :], fc1).then_inc(params, 16)
            sp.dma_start(fc1_in[:, 1, :], fc1).then_inc(params, 16)
            for h in range(2):
                sp.dma_start(fc2_in[C * h:C * h + C, :, :],
                             fc2.rearrange("(c t) r -> c t r", t=K * K)).then_inc(params, 16)
                sp.dma_start(expand_in[:, :, h, :],
                             expand.rearrange("(m o) c -> o m c", m=HALVES)).then_inc(params, 16)
                sp.dma_start(ln2[C * h:C * h + C, 0:1],
                             ln2_w.rearrange("(c a) -> c a", a=1)).then_inc(params, 16)
                sp.dma_start(ln2[C * h:C * h + C, 1:2],
                             ln2_b.rearrange("(c a) -> c a", a=1)).then_inc(params, 16)
            sp.dma_start(shrink_in[:, :], shrink).then_inc(params, 16)
            sp.dma_start(kept["gamma"][:, :], gamma.rearrange("(m o) -> o m", m=HALVES)).then_inc(params, 16)
            sp.dma_start(beta_in[:, :], beta.rearrange("(m o) -> o m", m=HALVES)).then_inc(params, 16)
            for i, v in enumerate((ln1_w, ln1_b)):
                sp.dma_start(kept["ln1_wb"][:, i, :],
                             v.rearrange("(a r) -> a r", a=1).to_broadcast([LN1, CR])).then_inc(params, 16)
            for n in range(2, LOADS):
                sp.wait_ge(x_spread, 4 * (n - 1))
                load(n)

        @block.gpsimd
        def _(pool):
            pool.memset(ident[:, :], 0.0).then_inc(ident_zero, 1)
            pool.wait_ge(ident_zero, 1)
            pool.affine_select(out=ident[:, :], in_=ident[:, :], compare_op=ALU.not_equal, fill=1.0,
                               base=0, pattern=[[-1, P]], channel_multiplier=1).then_inc(ident_ready, 1)

            def step(s, n, r, par):
                pool.wait_ge(high_ready, n + 1)
                pool.tensor_tensor(rest[:, :].rearrange("p (b i) -> p b i", b=B), line(s, r),
                                   line_hi[:, 1 - par, :, REACH:REACH + WP].bitcast(F32),
                                   ALU.subtract).then_inc(rest_ready, 1)

            for s in range(4):
                run(pool, s, lambda n, r, par: step(s, n, r, par))

        @block.scalar
        def _(act):
            def spread(n):
                act.wait_ge(x_loaded[n % 2], 32 * (n // 2 + 1))
                for g in range(2):
                    for p in range(2):
                        act.activation(
                            by_w[C * p:C * p + C, BG * g:BG * g + BG, ROWS_A_LOAD * n:ROWS_A_LOAD * (n + 1), :]
                            .rearrange("c b h i -> c b (h i)"),
                            stage[C * g:C * g + C, n % 2, :, :, :]
                            .rearrange("c b h (i p) -> c b (h i) p", p=2)[:, :, :, p],
                            ACT.Copy).then_inc(x_spread, 1)

            def copy_main(n, par):
                act.wait_ge(high_ready, n + 1)
                act.activation(main_sb[:, par, :], bank[par][:, 0:LINE], ACT.Copy).then_inc(main_copied, 1)

            def turn(r, j, hp, count):
                if count is not None:
                    act.wait_ge(line_done, count)
                for p in range(2):
                    o = by_h[C * hp:C * hp + C, :, :, :].rearrange("c b (i p) j -> c b i p j", p=2)
                    if isinstance(j, int):
                        dst = o[:, :, :, p, j]
                    else:
                        dst = o[:, :, :, p, bass.ds(j, 1)].rearrange("c b i a -> c b (i a)")
                    src = (by_w[C * p:C * p + C, :, r, :] if isinstance(r, int) else
                           by_w[C * p:C * p + C, :, bass.ds(r, 1), :].rearrange("c b a i -> c b (a i)"))
                    act.activation(dst, src, ACT.Copy).then_inc(turned, 1)

            spread(0)
            spread(1)
            for n in range(LOADS):
                with act.Fori(0, ROWS_A_LOAD // 2) as i:
                    for u in range(2):
                        copy_main(ROWS_A_LOAD * n + u + 2 * i, u)
                if n + 2 < LOADS:
                    spread(n + 2)
            turn(H - 1, HP - 1, 1, H)
            n0 = first[1]
            with act.Fori(0, counts[1] // 2) as i:
                for u in range(2):
                    copy_main(n0 + u + 2 * i, (n0 + u) % 2)
                    turn(i * -2 + (H - 2 - u), i * -1 + (HP - 1 - u), u, n0 + u + 1 + 2 * i)
            copy_main(first[2] - 1, (first[2] - 1) % 2)
            turn(0, 0, 0, first[2])
            for s in (2, 3):
                run(act, s, lambda n, r, par: copy_main(n, par))

        @block.vector
        def _(dve):
            dve.memset(taps[:, :, :, :].rearrange("p d o c -> p (d o c)"), 0.0)
            dve.memset(later, 0.0).then_inc(taps_zero, 1)
            dve.memset(line_hi[:, :, :, :].rearrange("p s b i -> p (s b i)").bitcast(F32), 0.0)
            dve.memset(line_lo[:, :, :, :].rearrange("p s b i -> p (s b i)").bitcast(F32), 0.0).then_inc(line_zero, 1)
            dve.memset(kept["pick"][:, :], 0.0)
            dve.memset(kept["mean_ce"][:, :], 1.0 / CE).then_inc(consts, 1)

            def split_taps(s):
                dve.wait_ge(taps_loaded[s], 64)
                flat = raw[s].rearrange("p d o c -> p d (o c)")
                dve.tensor_copy(taps_hi[:, s, :, :], flat).then_inc(taps_high, 1)
                dve.wait_ge(taps_high, s + 1)
                dve.tensor_tensor(taps_lo[:, s, :, :], flat, taps_hi[:, s, :, :].bitcast(F32),
                                  ALU.subtract).then_inc(taps_ready, 1)

            split_taps(0)

            def prepare():
                dve.wait_ge(consts, 1)
                dve.memset(kept["pick"][0:C, STAT_ROWS - 2:STAT_ROWS - 1], 1.0 / C)
                dve.memset(kept["pick"][C:P, STAT_ROWS - 1:STAT_ROWS], 1.0 / C)
                dve.wait_ge(ident_ready, 1)
                dve.tensor_tensor(kept["centre"][:, :], ident[:, 0:C], ident[:, C:P], ALU.add).then_inc(consts, 1)
                dve.wait_ge(consts, 2)
                dve.tensor_scalar(kept["centre"][:, :], kept["centre"][:, :], 1.0 / C, None, ALU.subtract)
                dve.wait_ge(params, 16 * N_PARAMS)
                dve.wait_ge(prep_mm, 1)
                dve.tensor_scalar(kept["fc1_t"][:, :], prep_ps[0][:, 0:CR], 1.0 / (H * W), None, ALU.mult)
                dve.tensor_copy(kept["fc2_t"][:, 0:4, :], prep_ps[1][0:CR, :].rearrange("r (t c) -> r t c", c=P)).then_inc(prep_ev, 1)
                for g in range(1, 7):
                    n = min(4, K * K - 4 * g)
                    dve.wait_ge(prep_mm, 1 + g)
                    dve.tensor_copy(kept["fc2_t"][:, 4 * g:4 * g + n, :],
                                    prep_ps[1 + g % 2][0:CR, 0:n * P].rearrange("r (t c) -> r t c", c=P)).then_inc(prep_ev, 1)
                dve.wait_ge(prep_mm, 8)
                dve.tensor_copy(kept["expand_t"][:, :, :], prep_ps[0][:, 0:HALVES * P].rearrange("p (m o) -> p m o", m=HALVES)).then_inc(prep_ev, 1)
                dve.wait_ge(prep_mm, 9)
                for d in range(2):
                    i = dve.tensor_copy(kept["shrink_t"][:, :, d, :], prep_ps[3][:, 0:HALVES * C].rearrange("p (m c) -> p m c", m=HALVES))
                i.then_inc(prep_ev, 1)
                dve.wait_ge(prep_mm, 10)
                dve.tensor_copy(kept["expand_bias"][:, :], prep_ps[0][:, 0:HALVES])
                dve.tensor_copy(kept["out_bias"][:, :], prep_ps[0][:, HALVES:HALVES + 1])
                dve.tensor_scalar(kept["expand_t"][:, :, :], kept["expand_t"][:, :, :], ln2[:, 0:1], None, ALU.mult)

            def step(s, n, r, par):
                x_line = line(s, r)
                new_hi = line_hi[:, 1 - par, :, REACH:REACH + WP]
                new_lo = line_lo[:, 1 - par, :, REACH:REACH + WP]
                as_lines = lambda t: t.rearrange("p (b i) -> p b i", b=B)
                dve.wait_ge(main_done, n + 1)
                dve.scalar_tensor_tensor(out=new_hi, in0=as_lines(main_ps[par][:, 0:LINE]), scalar=0.0,
                                         in1=x_line, op0=ALU.max, op1=ALU.add).then_inc(high_ready, 1)
                dve.wait_ge(main_copied, n + 1)
                dve.wait_ge(low_done, n + 1)
                dve.tensor_tensor(both[:, :], main_sb[:, par, :], low_ps[par][:, 0:LINE],
                                  ALU.add).then_inc(both_ready, 1)
                dve.wait_ge(rest_ready, n + 1)
                dve.wait_ge(both_ready, n + 1)
                dve.scalar_tensor_tensor(out=new_lo, in0=as_lines(both[:, :]), scalar=0.0,
                                         in1=as_lines(rest[:, :]), op0=ALU.max, op1=ALU.add).then_inc(low_ready, 1)
                dve.wait_ge(low_ready, n + 1)
                dve.tensor_tensor(x_line, new_hi.bitcast(F32), new_lo.bitcast(F32), ALU.add).then_inc(line_done, 1)

            for k in range(LOADS):
                dve.wait_ge(x_spread, 4 * (k + 1))
                with dve.Fori(0, ROWS_A_LOAD // 2) as i:
                    for u in range(2):
                        step(0, ROWS_A_LOAD * k + u + 2 * i, ROWS_A_LOAD * k + u + 2 * i, u)
                if k == 0:
                    for s in range(1, 4):
                        split_taps(s)
                if k == 1:
                    prepare()
            run(dve, 1, lambda n, r, par: step(1, n, r, par))
            slot = first[2] % 2
            dve.wait_ge(line_done, first[2])
            dve.memset(line_hi[:, slot, :, REACH:REACH + WP].bitcast(F32), 0.0)
            dve.memset(line_lo[:, slot, :, REACH:REACH + WP].bitcast(F32), 0.0).then_inc(line_zero, 1)
            dve.wait_ge(turned, 2 * H)
            for s in (2, 3):
                run(dve, s, lambda n, r, par: step(s, n, r, par))

        @block.tensor
        def _(pe):
            def step(s, n, r, par):
                if n is not None:
                    pe.wait_ge(high_ready, n)
                for d in range(OFFSETS):
                    mm = pe.matmul(main_ps[par][:, 0:LINE], taps_hi[:, s, d, :],
                                   line_hi[:, par, :, d:d + WP], start=(d == 0), stop=(d == OFFSETS - 1))
                mm.then_inc(main_done, 1)
                for d in range(OFFSETS):
                    pe.matmul(low_ps[par][:, 0:LINE], taps_lo[:, s, d, :],
                              line_hi[:, par, :, d:d + WP], start=(d == 0), stop=False)
                if n is not None:
                    pe.wait_ge(low_ready, n)
                for d in range(OFFSETS):
                    mm = pe.matmul(low_ps[par][:, 0:LINE], taps_hi[:, s, d, :],
                                   line_lo[:, par, :, d:d + WP], start=False, stop=(d == OFFSETS - 1))
                mm.then_inc(low_done, 1)

            def prepare():
                pe.wait_ge(params, 16 * N_PARAMS)
                pe.wait_ge(ident_ready, 1)
                pe.transpose(prep_ps[0][:, 0:CR], fc1_in[:, :, :].rearrange("r a c -> r (a c)"), ident[0:CR, 0:CR])
                for g in range(7):
                    if g >= 2:
                        pe.wait_ge(prep_ev, g - 1)
                    for t in range(4 * g, min(4 * g + 4, K * K)):
                        mm = pe.transpose(prep_ps[1 + g % 2][0:CR, (t % 4) * P:(t % 4) * P + P], fc2_in[:, t, :], ident[:, :])
                    mm.then_inc(prep_mm, 1)
                pe.wait_ge(prep_ev, 1)
                for m in range(HALVES):
                    mm = pe.transpose(prep_ps[0][:, m * P:(m + 1) * P],
                                      expand_in[:, m, :, :].rearrange("o a c -> o (a c)"), ident[:, :])
                mm.then_inc(prep_mm, 1)
                for m in range(HALVES):
                    mm = pe.transpose(prep_ps[3][:, m * C:(m + 1) * C], shrink_in[:, m * P:(m + 1) * P], ident[0:C, 0:C])
                mm.then_inc(prep_mm, 1)
                pe.wait_ge(prep_ev, 9)
                for m in range(HALVES):
                    pe.matmul(prep_ps[0][:, m:m + 1], kept["expand_t"][0:C, m, :], ln2[0:C, 1:2], start=True, stop=True)
                for m in range(HALVES):
                    mm = pe.matmul(prep_ps[0][:, HALVES:HALVES + 1],
                                   kept["shrink_t"][:, m, :, :].rearrange("p a c -> p (a c)"),
                                   beta_in[:, m:m + 1], start=(m == 0), stop=(m == HALVES - 1))
                mm.then_inc(prep_mm, 1)

            pe.wait_ge(line_zero, 1)
            pe.wait_ge(taps_ready, 1)
            for k in range(2):
                step(0, k or None, k, k)
            with pe.Fori(1, ROWS_A_LOAD) as i:
                for u in range(2):
                    step(0, u + 2 * i, None, u)
            prepare()
            with pe.Fori(ROWS_A_LOAD, H // 2) as i:
                for u in range(2):
                    step(0, u + 2 * i, None, u)
            pe.wait_ge(taps_ready, 4)
            run(pe, 1, lambda n, r, par: step(1, n, r, par))
            pe.wait_ge(line_zero, 2)
            for s in (2, 3):
                run(pe, s, lambda n, r, par: step(s, n, r, par))


def block_two(nc, bank, kept, out):
    by_h = kept["by_h"]
    conv_ps, stat_ps, wide_ps, exp_ps, out_ps = bank[0:2], bank[2], bank[3], bank[4:6], bank[6:8]
    with ExitStack() as ctx:
        def sb(name, shape, dt=F32):
            return ctx.enter_context(nc.sbuf_tensor(name, shape, dt))

        def sem(name):
            return ctx.enter_context(nc.semaphore(name))

        x_hi = sb("x_hi", [P, 2, XW, XJ], F32R)
        x_lo = sb("x_lo", [P, 2, XW, XJ], F32R)
        dyn_hi = sb("dyn_hi", [P, 2, KD * K, 2, C], F32R)
        dyn_lo = sb("dyn_lo", [P, 2, KD * K, 2, C], F32R)
        dyn_all = kept["dyn_all"]
        tap = sb("tap", [P, B, 2, KD * K])
        centred = sb("centred", [P, PIX])
        squares = sb("squares", [P, PIX])
        normed = sb("normed", [P, COLS * 2])
        wide = sb("wide", [P, HALVES, 2, PIX])
        result = squares[:, :].rearrange("p (j w) -> p j w", w=W)
        pooled = sb("pooled", [P, B])
        hid = sb("hid", [LN1, 4, CR])
        hst = sb("hst", [LN1, 4])
        hid_t = sb("hid_t", [CR, B])
        std = sb("std", [STAT_ROWS, 2, STAT_COLS])
        rstd_hi = sb("rstd_hi", [STAT_ROWS, STAT_COLS], F32R)
        rstd_lo = sb("rstd_lo", [STAT_ROWS, STAT_COLS], F32R)
        energy = sb("energy", [P, HALVES, 2])
        resp = sb("resp", [P, 6, HALVES])
        shrink_now = sb("shrink_now", [P, HALVES, C])
        eps_col = sb("eps_col", [P, 1])

        chain = sem("chain")
        eps_ready = sem("eps_ready")
        pool_mm = sem("pool_mm")
        pool_sd = sem("pool_sd")
        xhi_ready = sem("xhi_ready")
        xlo_ready = sem("xlo_ready")
        dyn_ready = sem("dyn_ready")
        pads = sem("pads")
        conv_done = sem("conv_done")
        conv_kept = sem("conv_kept")
        var_done = sem("var_done")
        std_ready = sem("std_ready")
        rstd_ready = sem("rstd_ready")
        wide_done = sem("wide_done")
        normed_ready = sem("normed_ready")
        exp_done = sem("exp_done")
        gelu_done = sem("gelu_done")
        energy_ready = sem("energy_ready")
        energy_sum = sem("energy_sum")
        resp_ready = sem("resp_ready")
        resp_mean = sem("resp_mean")
        shrink_ready = sem("shrink_ready")
        resp_step = sem("resp_step")
        rstd_step = sem("rstd_step")
        out_done = sem("out_done")
        result_ready = sem("result_ready")
        stored = sem("stored")

        def image(b):
            if isinstance(b, int):
                return by_h[:, b, :, :]
            return by_h[:, bass.ds(b, 1), :, :].rearrange("p a w j -> p (a w) j")

        def batches(engine, step):
            step(0, 0, True)
            with engine.Fori(0, (B - 2) // 2) as i:
                for u in range(2):
                    step(1 + u + 2 * i, (1 + u) % 2, False)
            step(B - 1, (B - 1) % 2, False)

        block = ctx.enter_context(nc.Block())

        @block.sync
        def _(sp):
            o = out.rearrange("b c (j p) w -> b p c j w", p=2)
            for b in range(B):
                sp.wait_ge(result_ready, CHUNKS * (b + 1))
                for p in range(2):
                    sp.dma_start(o[b, p], result[C * p:C * p + C, :, :]).then_inc(stored, 16)
            sp.wait_ge(stored, 32 * B)

        @block.scalar
        def _(act):
            def split_high(b, par):
                if not isinstance(b, int) or b >= 2:
                    act.wait_ge(conv_done, CHUNKS * (b - 1))
                act.activation(x_hi[:, par, 2:2 + W, 1:1 + HP], image(b), ACT.Copy).then_inc(xhi_ready, 1)

            act.wait_ge(pads, 1)
            split_high(0, 0)
            act.wait_ge(eps_ready, 1)
            act.wait_ge(chain, 5)
            act.activation(hst[:, 2:3], hst[:, 1:2], ACT.Sqrt, bias=eps_col[0:LN1, :], scale=1.0 / CR).then_inc(pool_sd, 1)

            def respond(b):
                act.wait_ge(energy_sum, b + 1)
                act.activation(resp[:, 1, :], resp[:, 0, :], ACT.Sqrt).then_inc(resp_ready, 1)

            def step(b, par, is_first, last=False):
                if not last:
                    split_high(b + 1, 1 - par)
                for q in range(CHUNKS):
                    act.wait_ge(conv_done, CHUNKS * b + q + 1)
                    if q == 0 and not is_first:
                        act.wait_ge(normed_ready, CHUNKS * b)
                        act.wait_ge(energy_ready, 4 * b)
                        act.wait_ge(var_done, b)
                    if q == 0 and (not isinstance(b, int) or b >= 2):
                        act.wait_ge(stored, 32 * (b - 1))
                    act.activation(centred[:, q * COLS:(q + 1) * COLS], conv_ps[q % 2][:, :], ACT.Copy)
                    act.activation(squares[:, q * COLS:(q + 1) * COLS], conv_ps[q % 2][:, :],
                                   ACT.Square).then_inc(conv_kept, 1)
                if not is_first:
                    respond(b - 1)
                act.wait_ge(var_done, b + 1)
                act.activation(std[:, 0, :], stat_ps[0:STAT_ROWS, 0:STAT_COLS], ACT.Sqrt,
                               bias=eps_col[0:STAT_ROWS, :]).then_inc(std_ready, 1)
                for q in range(CHUNKS):
                    for hp in range(2):
                        for m in range(HALVES):
                            e = (q * 2 + hp) * HALVES + m
                            act.wait_ge(exp_done, 4 * CHUNKS * b + e + 1)
                            if e == 0 and not is_first:
                                act.wait_ge(out_done, CHUNKS * b)
                            act.activation(wide[:, m, hp, q * COLS:(q + 1) * COLS], exp_ps[e % 2][:, :],
                                           ACT.Gelu, bias=kept["expand_bias"][:, m:m + 1]).then_inc(gelu_done, 1)
                act.wait_ge(gelu_done, 4 * CHUNKS * (b + 1))
                act.wait_ge(normed_ready, CHUNKS * (b + 1))
                for m in range(HALVES):
                    for hp in range(2):
                        if m + hp > 0:
                            act.wait_ge(energy_ready, 4 * b + 2 * m + hp)
                        act.activation(centred[:, :], wide[:, m, hp, :], ACT.Square,
                                       accum_out=energy[:, m, hp:hp + 1]).then_inc(energy_ready, 1)

            step(0, 0, True)
            with act.Fori(0, (B - 2) // 2) as i:
                for u in range(2):
                    step(1 + u + 2 * i, (1 + u) % 2, False)
            step(B - 1, (B - 1) % 2, False, True)
            respond(B - 1)

        @block.vector
        def _(dve):
            n_chain = [0]

            def link(ins):
                n_chain[0] += 1
                ins.then_inc(chain, 1)
                dve.wait_ge(chain, n_chain[0])

            dve.memset(eps_col[:, :], EPS).then_inc(eps_ready, 1)
            dve.memset(x_hi[:, :, :, :].rearrange("p s w j -> p (s w j)").bitcast(F32), 0.0)
            dve.memset(x_lo[:, :, :, :].rearrange("p s w j -> p (s w j)").bitcast(F32), 0.0).then_inc(pads, 1)
            dve.memset(tap[:, :, :, :].rearrange("p b o t -> p (b o t)"), 0.0)
            link(dve.tensor_reduce(pooled[:, :], by_h[:, :, :, :].rearrange("p b w j -> p b (w j)"), AX.X, ALU.add))
            dve.wait_ge(pool_mm, 1)
            link(dve.tensor_reduce(hst[:, 0:1], wide_ps[0:LN1, 0:CR], AX.X, ALU.add))
            link(dve.tensor_scalar(hst[:, 0:1], hst[:, 0:1], 1.0 / CR, None, ALU.mult))
            link(dve.tensor_scalar(hid[:, 0, :], wide_ps[0:LN1, 0:CR], hst[:, 0:1], None, ALU.subtract))
            link(dve.tensor_tensor_reduce(hid[:, 1, :], hid[:, 0, :], hid[:, 0, :], 1.0, 0.0, ALU.mult, ALU.add, hst[:, 1:2]))
            dve.wait_ge(pool_sd, 1)
            link(dve.reciprocal(hst[:, 3:4], hst[:, 2:3]))
            link(dve.scalar_tensor_tensor(out=hid[:, 2, :], in0=hid[:, 0, :], scalar=hst[:, 3:4],
                                          in1=kept["ln1_wb"][:, 0, :], op0=ALU.mult, op1=ALU.mult))
            link(dve.tensor_tensor(hid[:, 3, :], hid[:, 2, :], kept["ln1_wb"][:, 1, :], ALU.add))
            dve.wait_ge(pool_mm, 2)
            link(dve.tensor_copy(hid_t[:, :], wide_ps[0:CR, 0:B]))
            dve.wait_ge(pool_mm, 3)
            dyn = stat_ps[:, 0:K * K * B].rearrange("p (r s b) -> p b r s", r=K, s=K)
            t6 = tap[:, :, :, :].rearrange("p b o (d s) -> p b o d s", s=K)
            for pi in range(2):
                for po in range(2):
                    r0 = pi - po
                    d0 = 1 if r0 < 0 else 0
                    for d in range(d0, d0 + KD - abs(r0)):
                        last = dve.tensor_copy(t6[C * pi:C * pi + C, :, po, d, :], dyn[C * pi:C * pi + C, :, r0 + 2 * d, :])
            link(last)
            link(dve.tensor_copy(kept["spread"][:, :, :],
                                 kept["ident"][0:STAT_ROWS, 0:STAT_ROWS].rearrange("p (a o) -> p a o", o=1)
                                 .to_broadcast([STAT_ROWS, STAT_ROWS, C])))

            def prepare(b, par):
                if not isinstance(b, int) or b >= 2:
                    dve.wait_ge(conv_done, CHUNKS * (b - 1))
                dve.wait_ge(xhi_ready, b + 1)
                dve.tensor_tensor(x_lo[:, par, 2:2 + W, 1:1 + HP], image(b),
                                  x_hi[:, par, 2:2 + W, 1:1 + HP].bitcast(F32), ALU.subtract).then_inc(xlo_ready, 1)
                shape = [P, KD * K, 2, C]
                centre = kept["centre"][:, :].rearrange("p (a o c) -> p a o c", a=1, o=1).to_broadcast(shape)
                t = (tap[:, b, :, :] if isinstance(b, int) else
                     tap[:, bass.ds(b, 1), :, :].rearrange("p a o t -> p (a o) t"))
                t = t.rearrange("p o (t a) -> p t o a", a=1).to_broadcast(shape)
                dve.tensor_tensor(dyn_hi[:, par, :, :, :], centre, t, ALU.mult)
                if not isinstance(b, int) or b > 0:
                    dve.wait_ge(dyn_ready, 2 * b)
                dve.tensor_tensor(dyn_all[:, :, :, :], centre, t, ALU.mult).then_inc(dyn_ready, 1)
                dve.wait_ge(dyn_ready, 2 * b + 1)
                dve.tensor_tensor(dyn_lo[:, par, :, :, :], dyn_all[:, :, :, :],
                                  dyn_hi[:, par, :, :, :].bitcast(F32), ALU.subtract).then_inc(dyn_ready, 1)

            def respond(b):
                dve.wait_ge(resp_mean, b + 1)
                dve.tensor_scalar(resp[:, 2, 0:1], wide_ps[:, 0:1], EPS, None, ALU.add).then_inc(resp_step, 1)
                dve.wait_ge(resp_step, 4 * b + 1)
                dve.reciprocal(resp[:, 3, 0:1], resp[:, 2, 0:1]).then_inc(resp_step, 1)
                dve.wait_ge(resp_step, 4 * b + 2)
                dve.scalar_tensor_tensor(out=resp[:, 4, :], in0=resp[:, 1, :], scalar=resp[:, 3, 0:1],
                                         in1=kept["gamma"][:, :], op0=ALU.mult, op1=ALU.mult).then_inc(resp_step, 1)
                dve.wait_ge(resp_step, 4 * b + 3)
                dve.tensor_scalar(resp[:, 5, :], resp[:, 4, :], 1.0, None, ALU.add).then_inc(resp_step, 1)
                dve.wait_ge(resp_step, 4 * b + 4)
                for m in range(HALVES):
                    last = dve.tensor_scalar(shrink_now[:, m, :], kept["shrink_t"][:, m, 0, :], resp[:, 5, m:m + 1],
                                             None, ALU.mult)
                last.then_inc(shrink_ready, 1)

            def finish(b):
                for q in range(CHUNKS):
                    dve.wait_ge(out_done, CHUNKS * b + q + 1)
                    dve.scalar_tensor_tensor(
                        out=result[:, :, q * CW:(q + 1) * CW].rearrange("p j w -> p w j"),
                        in0=out_ps[q % 2][:, :].rearrange("p (w j) -> p w j", w=CW),
                        scalar=kept["out_bias"][:, :], in1=image(b)[:, q * CW:(q + 1) * CW, :],
                        op0=ALU.add, op1=ALU.add).then_inc(result_ready, 1)

            def step(b, par, is_first, last=False):
                if not last:
                    prepare(b + 1, 1 - par)
                if not is_first:
                    respond(b - 1)
                dve.wait_ge(std_ready, b + 1)
                dve.reciprocal(std[:, 1, :], std[:, 0, :]).then_inc(rstd_step, 1)
                dve.wait_ge(rstd_step, 2 * b + 1)
                dve.tensor_copy(rstd_hi[:, :], std[:, 1, :]).then_inc(rstd_step, 1)
                dve.wait_ge(rstd_step, 2 * b + 2)
                dve.tensor_tensor(rstd_lo[:, :], std[:, 1, :], rstd_hi[:, :].bitcast(F32),
                                  ALU.subtract).then_inc(rstd_ready, 1)
                if not is_first:
                    finish(b - 1)
                for q in range(CHUNKS):
                    dve.wait_ge(wide_done, CHUNKS * b + q + 1)
                    if q >= 2:
                        dve.wait_ge(exp_done, 4 * CHUNKS * b + 4 * (q - 1))
                    dve.tensor_tensor(normed[:, (q % 2) * COLS:(q % 2 + 1) * COLS],
                                      centred[:, q * COLS:(q + 1) * COLS], wide_ps[:, :],
                                      ALU.mult).then_inc(normed_ready, 1)
                dve.wait_ge(energy_ready, 4 * (b + 1))
                dve.tensor_tensor(resp[:, 0, :], energy[:, :, 0], energy[:, :, 1], ALU.add).then_inc(energy_sum, 1)

            prepare(0, 0)
            step(0, 0, True)
            with dve.Fori(0, (B - 2) // 2) as i:
                for u in range(2):
                    step(1 + u + 2 * i, (1 + u) % 2, False)
            step(B - 1, (B - 1) % 2, False, True)
            respond(B - 1)
            dve.wait_ge(stored, 32 * (B - 1))
            finish(B - 1)

        @block.tensor
        def _(pe):
            pe.wait_ge(chain, 1)
            pe.matmul(wide_ps[0:LN1, 0:CR], pooled[:, :], kept["fc1_t"][:, :], start=True, stop=True).then_inc(pool_mm, 1)
            pe.wait_ge(chain, 8)
            pe.transpose(wide_ps[0:CR, 0:B], hid[:, 3, :], kept["ident"][0:LN1, 0:LN1]).then_inc(pool_mm, 1)
            pe.wait_ge(chain, 9)
            for t in range(K * K):
                mm = pe.matmul(stat_ps[:, t * B:(t + 1) * B], kept["fc2_t"][:, t, :], hid_t[:, :], start=True, stop=True)
            mm.then_inc(pool_mm, 1)

            def respond(b):
                pe.wait_ge(resp_ready, b + 1)
                for m in range(HALVES):
                    mm = pe.matmul(wide_ps[:, 0:1], kept["mean_ce"][:, :], resp[:, 1, m:m + 1],
                                   start=(m == 0), stop=(m == HALVES - 1))
                mm.then_inc(resp_mean, 1)

            def shrink(b):
                pe.wait_ge(shrink_ready, b + 1)
                for q in range(CHUNKS):
                    if q >= 2:
                        pe.wait_ge(result_ready, CHUNKS * b + q - 1)
                    for hp in range(2):
                        for m in range(HALVES):
                            mm = pe.matmul(out_ps[q % 2][C * hp:C * hp + C, :], shrink_now[:, m, :],
                                           wide[:, m, hp, q * COLS:(q + 1) * COLS],
                                           start=(m == 0), stop=(m == HALVES - 1))
                    mm.then_inc(out_done, 1)

            def step(b, par, is_first):
                pe.wait_ge(dyn_ready, 2 * b + 2)
                pe.wait_ge(xlo_ready, b + 1)
                for q in range(CHUNKS):
                    if not is_first or q >= 2:
                        pe.wait_ge(conv_kept, CHUNKS * b + q - 1)
                    n = 0
                    for d in range(KD):
                        for s in range(K):
                            t = d * K + s
                            for w, v in ((dyn_hi, x_hi), (dyn_hi, x_lo), (dyn_lo, x_hi)):
                                mm = pe.matmul(conv_ps[q % 2][:, :],
                                               w[:, par, t, :, :].rearrange("p o c -> p (o c)"),
                                               v[:, par, q * CW + s:(q + 1) * CW + s, d:d + HP],
                                               start=(n == 0), stop=(n == 3 * KD * K - 1))
                                n += 1
                    mm.then_inc(conv_done, 1)
                if not is_first:
                    respond(b - 1)
                pe.wait_ge(conv_kept, CHUNKS * (b + 1))
                for k in range(STATS):
                    mm = pe.matmul(stat_ps[0:STAT_ROWS, 0:STAT_COLS],
                                   kept["pick"][:, STAT_ROWS - 2 - 2 * k:2 * STAT_ROWS - 2 - 2 * k],
                                   squares[:, k * STAT_COLS:(k + 1) * STAT_COLS], start=(k == 0), stop=(k == STATS - 1))
                mm.then_inc(var_done, 1)
                if not is_first:
                    shrink(b - 1)
                pe.wait_ge(rstd_ready, b + 1)

                def widen(q):
                    if q > 0:
                        pe.wait_ge(normed_ready, CHUNKS * b + q)
                    for k in range(q * STATS // CHUNKS, (q + 1) * STATS // CHUNKS):
                        o = wide_ps[:, (k % 4) * STAT_COLS:(k % 4 + 1) * STAT_COLS]
                        w = kept["spread"][:, 2 * k:2 * k + 2, :].rearrange("p a c -> p (a c)")
                        pe.matmul(o, w, rstd_hi[:, :], start=True, stop=False)
                        mm = pe.matmul(o, w, rstd_lo[:, :], start=False, stop=True)
                    mm.then_inc(wide_done, 1)

                widen(0)
                for q in range(CHUNKS):
                    pe.wait_ge(normed_ready, CHUNKS * b + q + 1)
                    if q + 1 < CHUNKS:
                        widen(q + 1)
                    for hp in range(2):
                        for m in range(HALVES):
                            e = (q * 2 + hp) * HALVES + m
                            if not is_first or e >= 2:
                                pe.wait_ge(gelu_done, 4 * CHUNKS * b + e - 1)
                            pe.matmul(exp_ps[e % 2][:, :], kept["expand_t"][C * hp:C * hp + C, m, :],
                                      normed[C * hp:C * hp + C, (q % 2) * COLS:(q % 2 + 1) * COLS],
                                      start=True, stop=True).then_inc(exp_done, 1)

            batches(pe, step)
            respond(B - 1)
            shrink(B - 1)


_INS = ['x', 'L0_conv_k_td', 'L0_conv_k_dt', 'L0_conv_k_lr', 'L0_conv_k_rl', 'L1_conv_w_fc1', 'L1_conv_ln1_w',
        'L1_conv_ln1_b', 'L1_conv_w_fc2', 'L1_conv_ln2_w', 'L1_conv_ln2_b', 'L1_conv_w_expand',
        'L1_conv_w_shrink', 'L1_conv_grn_gamma', 'L1_conv_grn_beta']
_OUT = ((8, 64, 64, 64), 'float32')


def kernel(**inputs):
    import numpy as _np
    import concourse.bacc as _bacc
    from concourse import mybir as _mybir
    from concourse.bass_utils import run_bass_kernel_spmd as _run

    nc = _bacc.Bacc("TRN2", target_bir_lowering=False, num_devices=1)
    arrays, args = {}, []
    for name in _INS:
        a = _np.ascontiguousarray(inputs[name])
        arrays[f"in_{name}_dram"] = a
        args.append(nc.dram_tensor(f"in_{name}_dram", a.shape, _mybir.dt.from_np(a.dtype), kind="ExternalInput").ap())
    shape, dtype = _OUT
    args.append(nc.dram_tensor("out_0_dram", shape, _mybir.dt.from_np(_np.dtype(dtype)), kind="ExternalOutput").ap())
    build(nc, *args)
    r = _run(nc, [arrays], core_ids=[0])
    return r.results[0]["out_0_dram"]
```

```python
from contextlib import ExitStack

import concourse.bass as bass
from concourse import mybir

F32 = mybir.dt.float32
F32R = mybir.dt.float32r
ALU = mybir.AluOpType
ACT = mybir.ActivationFunctionType
AX = mybir.AxisListType

P = 128
B, C, H, W = 8, 64, 64, 64
TAPS = 9
REACH = 2
OFFSETS = 2 * REACH + 1
WP, HP = W // 2, H // 2
PADDED = WP + 2 * REACH
LINE = B * WP
UNROLL = 12
ROWS_A_LOAD = 4
STAGES = 3
LOADS = H // ROWS_A_LOAD
BG = B // 2

K = 5
KD = 3
EDGE = (0, K - 1)
NE = len(EDGE)
CR, CE = C // 4, 4 * C
HALVES = CE // P
EPS = 1e-6
LN1 = 8
PIX = W * HP
CHUNKS = 4
CW = W // CHUNKS
COLS = PIX // CHUNKS
STAT_COLS = 128
STATS = PIX // STAT_COLS
STAT_ROWS = 2 * STATS
XW, XJ = W + K - 1, HP + 2


def build(nc, x, k_td, k_dt, k_lr, k_rl, fc1, ln1_w, ln1_b, fc2, ln2_w, ln2_b,
          expand, shrink, gamma, beta, out):
    with ExitStack() as ctx:
        ctx.enter_context(nc.allow_non_contiguous_dma(reason="small parameters and rows of images"))
        bank = [ctx.enter_context(nc.psum_tensor(f"bank{i}", [P, 512], F32)) for i in range(8)]

        def sb(name, shape, dt=F32):
            return ctx.enter_context(nc.sbuf_tensor(name, shape, dt))

        kept = dict(
            by_h=sb("by_h", [P, B, W, HP]),
            ident=sb("ident", [P, P]),
            centre=sb("centre", [P, C]),
            centre_both=sb("centre_both", [P, 2, C]),
            line_sum=sb("line_sum", [P, B, HP]),
            pick=sb("pick", [P, 2 * STAT_ROWS - 2]),
            mean_ce=sb("mean_ce", [P, 1]),
            fc1_t=sb("fc1_t", [P, CR]),
            ln1_wb=sb("ln1_wb", [LN1, 2, CR]),
            expand_t=sb("expand_t", [P, HALVES, 2, P]),
            expand_bias=sb("expand_bias", [P, HALVES]),
            shrink_t=sb("shrink_t", [P, HALVES, C]),
            gamma=sb("gamma", [P, HALVES]),
            out_bias=sb("out_bias", [P, 1]),
        )
        at = -(-nc.sbuf_base // 32) * 32
        full_bytes = 4 * KD * NE * P
        sb("slab", [P, max(K * K * P, KD * NE * P + STAT_ROWS * C + STAT_COLS + HALVES * C)])
        kept["fc2_t"] = nc.alloc_sbuf_tensor_at("fc2_t", [CR, K * K, P], F32, offset=at)
        kept["dyn_all"] = nc.alloc_sbuf_tensor_at("dyn_all", [P, KD * NE, 2, C], F32, offset=at)
        spread_bytes = 4 * STAT_ROWS * C
        rstd_bytes = 4 * STAT_COLS
        kept["spread"] = nc.alloc_sbuf_tensor_at("spread", [2 * STAT_ROWS, STAT_ROWS, C], F32R,
                                                 offset=at + full_bytes)
        kept["rstd_parts"] = nc.alloc_sbuf_tensor_at("rstd_parts", [2 * STAT_ROWS, STAT_COLS], F32R,
                                                     offset=at + full_bytes + spread_bytes)
        kept["shrink_now"] = nc.alloc_sbuf_tensor_at("shrink_now", [P, HALVES, C], F32,
                                                     offset=at + full_bytes + spread_bytes + rstd_bytes)
        scans(nc, bank, kept, x, (k_td, k_dt, k_lr, k_rl), fc1, ln1_w, ln1_b, fc2, ln2_w, ln2_b,
              expand, shrink, gamma, beta)
        block_two(nc, bank, kept, out)


def scans(nc, bank, kept, x, kernels, fc1, ln1_w, ln1_b, fc2, ln2_w, ln2_b,
          expand, shrink, gamma, beta):
    by_h, ident = kept["by_h"], kept["ident"]
    main_ps, low_ps, prep_ps = bank[0:2], bank[2:4], bank[4:8]
    with ExitStack() as ctx:
        def sb(name, shape, dt=F32):
            return ctx.enter_context(nc.sbuf_tensor(name, shape, dt))

        def sem(name):
            return ctx.enter_context(nc.semaphore(name))

        by_w = sb("by_w", [P, B, H, WP])
        stage = sb("stage", [P, STAGES, BG, ROWS_A_LOAD, W])
        taps = sb("taps", [P, OFFSETS, 2, C])
        taps_hi = sb("taps_hi", [P, 4, OFFSETS, P], F32R)
        taps_lo = sb("taps_lo", [P, 4, OFFSETS, P], F32R)
        line_hi = sb("line_hi", [P, 2, B, PADDED], F32R)
        line_lo = sb("line_lo", [P, 2, B, PADDED], F32R)
        main_sb = sb("main_sb", [P, 2, LINE])
        rest = sb("rest", [P, LINE])
        fc1_in = sb("fc1_in", [CR, 2, C])
        fc2_in = sb("fc2_in", [P, K * K, CR])
        expand_in = sb("expand_in", [P, HALVES, 2, C])
        shrink_in = sb("shrink_in", [C, CE])
        ln2 = sb("ln2", [P, 2])
        beta_in = sb("beta_in", [P, HALVES])
        later = by_h[:, 0, :, :].rearrange("p w j -> p (w j)")[:, 0:3 * OFFSETS * P]
        raw = [taps[:, :, :, :]] + [
            later.rearrange("p (s d o c) -> p s d o c", s=3, d=OFFSETS, o=2)[:, n, :, :, :] for n in range(3)]

        x_loaded = [sem(f"x_loaded{i}") for i in range(STAGES)]
        x_spread = sem("x_spread")
        taps_zero = sem("taps_zero")
        taps_loaded = [sem(f"taps_loaded{i}") for i in range(4)]
        taps_high = sem("taps_high")
        taps_ready = sem("taps_ready")
        line_zero = sem("line_zero")
        main_done = sem("main_done")
        low_done = sem("low_done")
        high_ready = sem("high_ready")
        low_ready = sem("low_ready")
        main_copied = sem("main_copied")
        rest_ready = sem("rest_ready")
        both_ready = sem("both_ready")
        line_done = sem("line_done")
        summed = sem("summed")
        turned = sem("turned")
        params = sem("params")
        ident_zero = sem("ident_zero")
        ident_ready = sem("ident_ready")
        prep_mm = sem("prep_mm")
        prep_ev = sem("prep_ev")
        consts = sem("consts")

        N_PARAMS = 15

        counts = [H, H - 1, W, W - 1]
        first = [sum(counts[:s]) for s in range(4)]

        def line(s, r):
            image = by_w if s < 2 else by_h
            if isinstance(r, int):
                return image[:, :, r, :]
            return image[:, :, bass.ds(r, 1), :].rearrange("p b a i -> p b (a i)")

        head = [n % UNROLL for n in counts]

        def run(engine, s, step):
            for k in range(head[s]):
                step(s, k, (first[s] + k) % 2)
            with engine.Fori(0, counts[s] // UNROLL) as i:
                for u in range(UNROLL):
                    step(s, UNROLL * i + (head[s] + u), (first[s] + head[s] + u) % 2)

        def line_of(s, k):
            return line(s, k if s % 2 == 0 else k * -1 + (counts[s] - 1))

        block = ctx.enter_context(nc.Block())

        @block.sync
        def _(sp):
            def load(n):
                for g in range(2):
                    sp.dma_start(
                        stage[C * g:C * g + C, n % STAGES, :, :, :].rearrange("c b h w -> c b (h w)"),
                        x[BG * g:BG * g + BG, :, ROWS_A_LOAD * n:ROWS_A_LOAD * (n + 1), :]
                        .rearrange("b c h w -> c b (h w)")).then_inc(x_loaded[n % STAGES], 16)

            def load_taps(s):
                k = kernels[s].rearrange("t i o -> i t o")
                for pi in range(2):
                    for po in range(2):
                        lo = pi - po
                        d0 = 1 if lo < 0 else 0
                        n = OFFSETS - abs(lo)
                        t0 = lo + 2 * d0
                        sp.dma_start(raw[s][C * pi:C * pi + C, d0:d0 + n, po, :],
                                     k[:, t0:t0 + 2 * n - 1:2, :]).then_inc(taps_loaded[s], 16)

            load(0)
            sp.wait_ge(taps_zero, 1)
            load_taps(0)
            for n in range(1, STAGES):
                load(n)
            for s in range(1, 4):
                load_taps(s)
            sp.dma_start(fc1_in[:, 0, :], fc1).then_inc(params, 16)
            sp.dma_start(fc1_in[:, 1, :], fc1).then_inc(params, 16)
            for h in range(2):
                sp.dma_start(fc2_in[C * h:C * h + C, :, :],
                             fc2.rearrange("(c t) r -> c t r", t=K * K)).then_inc(params, 16)
                sp.dma_start(expand_in[:, :, h, :],
                             expand.rearrange("(m o) c -> o m c", m=HALVES)).then_inc(params, 16)
                sp.dma_start(ln2[C * h:C * h + C, 0:1],
                             ln2_w.rearrange("(c a) -> c a", a=1)).then_inc(params, 16)
                sp.dma_start(ln2[C * h:C * h + C, 1:2],
                             ln2_b.rearrange("(c a) -> c a", a=1)).then_inc(params, 16)
            sp.dma_start(shrink_in[:, :], shrink).then_inc(params, 16)
            sp.dma_start(kept["gamma"][:, :], gamma.rearrange("(m o) -> o m", m=HALVES)).then_inc(params, 16)
            sp.dma_start(beta_in[:, :], beta.rearrange("(m o) -> o m", m=HALVES)).then_inc(params, 16)
            for i, v in enumerate((ln1_w, ln1_b)):
                sp.dma_start(kept["ln1_wb"][:, i, :],
                             v.rearrange("(a r) -> a r", a=1).to_broadcast([LN1, CR])).then_inc(params, 16)
            for n in range(STAGES, LOADS):
                sp.wait_ge(x_spread, 4 * (n - STAGES + 1))
                load(n)

        @block.gpsimd
        def _(pool):
            pool.memset(ident[:, :], 0.0).then_inc(ident_zero, 1)
            pool.wait_ge(ident_zero, 1)
            pool.affine_select(out=ident[:, :], in_=ident[:, :], compare_op=ALU.not_equal, fill=1.0,
                               base=0, pattern=[[-1, P]], channel_multiplier=1).then_inc(ident_ready, 1)

            def step(s, k, par):
                n = first[s] + k
                x_line = line_of(s, k)
                pool.wait_ge(high_ready, n + 1)
                pool.tensor_tensor(rest[:, :].rearrange("p (b i) -> p b i", b=B), x_line,
                                   line_hi[:, 1 - par, :, REACH:REACH + WP].bitcast(F32),
                                   ALU.subtract).then_inc(rest_ready, 1)

            def add_line(n, last_line):
                pool.wait_ge(line_done, n)
                pool.wait_ge(summed, n - first[3])
                pool.tensor_tensor(line_sum, line_sum, last_line, ALU.add).then_inc(summed, 1)

            def step_and_sum(s, k, par):
                step(s, k, par)
                if not isinstance(k, int) or k > 0:
                    add_line(first[s] + k, line(s, k * -1 + counts[s]))

            for s in range(3):
                run(pool, s, step)
            line_sum = kept["line_sum"][:, :, :]
            pool.wait_ge(line_done, first[3])
            pool.tensor_copy(line_sum, line(3, W - 1)).then_inc(summed, 1)
            run(pool, 3, step_and_sum)
            add_line(first[3] + counts[3], line(3, 0))

        @block.scalar
        def _(act):
            def spread(i, n, part):
                g, p, v = part // 2, part % 2, n % STAGES
                load = STAGES * i + n
                rows = (by_w[:, :, ROWS_A_LOAD * load:ROWS_A_LOAD * (load + 1), :] if isinstance(i, int) else
                        by_w[:, :, bass.ds(ROWS_A_LOAD * load, ROWS_A_LOAD), :])
                if part == 0:
                    act.wait_ge(x_loaded[v], 32 * i + 32 * (n // STAGES + 1))
                act.activation(
                    rows[C * p:C * p + C, BG * g:BG * g + BG, :, :].rearrange("c b h i -> c b (h i)"),
                    stage[C * g:C * g + C, v, :, :, :]
                    .rearrange("c b h (i p) -> c b (h i) p", p=2)[:, :, :, p],
                    ACT.Copy).then_inc(x_spread, 1)

            def copy_main(n, par):
                act.wait_ge(main_done, n + 1)
                act.activation(main_sb[:, par, :], bank[par][:, 0:LINE], ACT.Copy).then_inc(main_copied, 1)

            def turn(r, j, hp, count):
                if count is not None:
                    act.wait_ge(line_done, count)
                for p in range(2):
                    o = by_h[C * hp:C * hp + C, :, :, :].rearrange("c b (i p) j -> c b i p j", p=2)
                    if isinstance(j, int):
                        dst = o[:, :, :, p, j]
                    else:
                        dst = o[:, :, :, p, bass.ds(j, 1)].rearrange("c b i a -> c b (i a)")
                    src = (by_w[C * p:C * p + C, :, r, :] if isinstance(r, int) else
                           by_w[C * p:C * p + C, :, bass.ds(r, 1), :].rearrange("c b a i -> c b (a i)"))
                    act.activation(dst, src, ACT.Copy).then_inc(turned, 1)

            for n in range(STAGES):
                for part in range(4):
                    spread(0, n, part)
            for k in range(head[0]):
                copy_main(k, k % 2)
                spread(0, STAGES, k)
            rounds = counts[0] // UNROLL
            with act.Fori(0, rounds - 1) as i:
                for u in range(UNROLL):
                    copy_main(UNROLL * i + (head[0] + u), u % 2)
                    spread(i, STAGES + 1 + u // 4, u % 4)
            for k in range(H - UNROLL, H):
                copy_main(k, k % 2)

            def dt_step(i, u):
                copy_main(first[1] + u + UNROLL * i, (first[1] + u) % 2)
                turn(i * -UNROLL + (H - u), i * (-UNROLL // 2) + (H - u) // 2, (H - u) % 2,
                     first[1] + u - 1 + UNROLL * i)

            copy_main(first[1], first[1] % 2)
            for u in range(1, head[1]):
                dt_step(0, u)
            with act.Fori(0, counts[1] // UNROLL) as i:
                for u in range(UNROLL):
                    dt_step(i, head[1] + u)
            turn(1, 0, 1, first[2] - 1)
            turn(0, 0, 0, first[2])
            for s in (2, 3):
                run(act, s, lambda s, k, par: copy_main(first[s] + k, par))

        @block.vector
        def _(dve):
            dve.memset(taps[:, :, :, :].rearrange("p d o c -> p (d o c)"), 0.0)
            dve.memset(later, 0.0).then_inc(taps_zero, 1)
            dve.memset(line_hi[:, :, :, :].rearrange("p s b i -> p (s b i)").bitcast(F32), 0.0)
            dve.memset(line_lo[:, :, :, :].rearrange("p s b i -> p (s b i)").bitcast(F32), 0.0).then_inc(line_zero, 1)
            dve.memset(kept["pick"][:, :], 0.0)
            dve.memset(kept["mean_ce"][:, :], 1.0 / CE).then_inc(consts, 1)

            def split_taps(s):
                dve.wait_ge(taps_loaded[s], 64)
                flat = raw[s].rearrange("p d o c -> p d (o c)")
                dve.tensor_copy(taps_hi[:, s, :, :], flat).then_inc(taps_high, 1)
                dve.wait_ge(taps_high, s + 1)
                dve.tensor_tensor(taps_lo[:, s, :, :], flat, taps_hi[:, s, :, :].bitcast(F32),
                                  ALU.subtract).then_inc(taps_ready, 1)

            split_taps(0)

            def prepare():
                dve.wait_ge(consts, 1)
                dve.memset(kept["pick"][0:C, STAT_ROWS - 2:STAT_ROWS - 1], 1.0 / C)
                dve.memset(kept["pick"][C:P, STAT_ROWS - 1:STAT_ROWS], 1.0 / C)
                dve.wait_ge(ident_ready, 1)
                dve.tensor_tensor(kept["centre"][:, :], ident[:, 0:C], ident[:, C:P], ALU.add).then_inc(consts, 1)
                dve.wait_ge(consts, 2)
                dve.tensor_scalar(kept["centre"][:, :], kept["centre"][:, :], 1.0 / C, None, ALU.subtract)
                for hp in range(2):
                    dve.memset(kept["expand_t"][C * (1 - hp):C * (1 - hp) + C, :, hp, :], 0.0)
                dve.memset(kept["centre_both"][:, :, :], 0.0).then_inc(consts, 1)
                dve.wait_ge(consts, 3)
                for hp in range(2):
                    half = slice(C * hp, C * hp + C)
                    dve.tensor_scalar(kept["centre_both"][half, hp, :], ident[half, half], 1.0 / C, None, ALU.subtract)
                dve.wait_ge(params, 16 * N_PARAMS)
                dve.wait_ge(prep_mm, 1)
                dve.tensor_scalar(kept["fc1_t"][:, :], prep_ps[0][:, 0:CR], 1.0 / (H * W), None, ALU.mult)
                dve.tensor_copy(kept["fc2_t"][:, 0:4, :], prep_ps[1][0:CR, :].rearrange("r (t c) -> r t c", c=P)).then_inc(prep_ev, 1)
                for g in range(1, 7):
                    n = min(4, K * K - 4 * g)
                    dve.wait_ge(prep_mm, 1 + g)
                    dve.tensor_copy(kept["fc2_t"][:, 4 * g:4 * g + n, :],
                                    prep_ps[1 + g % 2][0:CR, 0:n * P].rearrange("r (t c) -> r t c", c=P)).then_inc(prep_ev, 1)
                dve.wait_ge(prep_mm, 8)
                for hp in range(2):
                    half = slice(C * hp, C * hp + C)
                    i = dve.tensor_copy(kept["expand_t"][half, :, hp, :],
                                        prep_ps[0][half, 0:HALVES * P].rearrange("p (m o) -> p m o", m=HALVES))
                i.then_inc(prep_ev, 1)
                dve.wait_ge(prep_mm, 9)
                dve.tensor_copy(kept["shrink_t"][:, :, :], prep_ps[3][:, 0:HALVES * C].rearrange(
                    "p (m c) -> p m c", m=HALVES)).then_inc(prep_ev, 1)
                dve.wait_ge(prep_mm, 10)
                dve.tensor_copy(kept["expand_bias"][:, :], prep_ps[0][:, 0:HALVES])
                dve.tensor_copy(kept["out_bias"][:, :], prep_ps[0][:, HALVES:HALVES + 1])
                dve.tensor_scalar(kept["expand_t"][:, :, :, :], kept["expand_t"][:, :, :, :], ln2[:, 0:1], None, ALU.mult)

            def keep_line(s, k, par):
                part = slice(REACH, REACH + WP)
                dve.wait_ge(low_ready, first[s] + k + 1)
                dve.tensor_tensor(line_of(s, k), line_hi[:, 1 - par, :, part].bitcast(F32),
                                  line_lo[:, 1 - par, :, part].bitcast(F32), ALU.add).then_inc(line_done, 1)

            as_lines = lambda t: t.rearrange("p (b i) -> p b i", b=B)

            def high(s, k, par):
                n = first[s] + k
                x_line = line_of(s, k)
                dve.lower_ap(x_line)
                if not isinstance(n, int) or n >= 2:
                    dve.wait_ge(line_done, n - 1)
                dve.wait_ge(main_copied, n + 1)
                dve.scalar_tensor_tensor(out=line_hi[:, 1 - par, :, REACH:REACH + WP],
                                         in0=as_lines(main_ps[par][:, 0:LINE]), scalar=0.0,
                                         in1=x_line, op0=ALU.max, op1=ALU.add).then_inc(high_ready, 1)

            def low(s, k, par):
                n = first[s] + k
                product = as_lines(low_ps[par][:, 0:LINE])
                dve.wait_ge(low_done, n + 1)
                dve.tensor_tensor(product, as_lines(main_sb[:, par, :]), product, ALU.add).then_inc(both_ready, 1)
                dve.wait_ge(rest_ready, n + 1)
                dve.wait_ge(both_ready, n + 1)
                dve.scalar_tensor_tensor(out=line_lo[:, 1 - par, :, REACH:REACH + WP], in0=product, scalar=0.0,
                                         in1=as_lines(rest[:, :]), op0=ALU.max, op1=ALU.add).then_inc(low_ready, 1)

            def low_then_high(s, k, par):
                low(s, k, par)
                high(s, k + 1, 1 - par)
                keep_line(s, k, par)

            def scan(s):
                high(s, 0, first[s] % 2)
                for k in range(head[s] - 1):
                    low_then_high(s, k, (first[s] + k) % 2)
                with dve.Fori(0, counts[s] // UNROLL) as i:
                    if s == 0:
                        dve.wait_ge(x_spread, UNROLL * i + (head[0] + UNROLL))
                    for u in range(UNROLL):
                        low_then_high(s, UNROLL * i + (head[s] - 1 + u), (first[s] + head[s] - 1 + u) % 2)
                low(s, counts[s] - 1, (first[s] + counts[s] - 1) % 2)
                keep_line(s, counts[s] - 1, (first[s] + counts[s] - 1) % 2)

            dve.wait_ge(x_spread, ROWS_A_LOAD)
            for s in range(1, 4):
                split_taps(s)
            prepare()
            scan(0)
            scan(1)
            slot = first[2] % 2
            dve.wait_ge(line_done, first[2])
            dve.memset(line_hi[:, slot, :, REACH:REACH + WP].bitcast(F32), 0.0)
            dve.memset(line_lo[:, slot, :, REACH:REACH + WP].bitcast(F32), 0.0).then_inc(line_zero, 1)
            dve.wait_ge(turned, 2 * H)
            scan(2)
            scan(3)

        @block.tensor
        def _(pe):
            def step(s, k, par):
                n = first[s] + k
                if not isinstance(n, int) or n > 0:
                    pe.wait_ge(high_ready, n)
                for d in range(OFFSETS):
                    mm = pe.matmul(main_ps[par][:, 0:LINE], taps_hi[:, s, d, :],
                                   line_hi[:, par, :, d:d + WP], start=(d == 0), stop=(d == OFFSETS - 1))
                mm.then_inc(main_done, 1)
                for d in range(OFFSETS):
                    pe.matmul(low_ps[par][:, 0:LINE], taps_lo[:, s, d, :],
                              line_hi[:, par, :, d:d + WP], start=(d == 0), stop=False)
                if not isinstance(n, int) or n > 0:
                    pe.wait_ge(low_ready, n)
                for d in range(OFFSETS):
                    mm = pe.matmul(low_ps[par][:, 0:LINE], taps_hi[:, s, d, :],
                                   line_lo[:, par, :, d:d + WP], start=False, stop=(d == OFFSETS - 1))
                mm.then_inc(low_done, 1)

            def prepare():
                pe.wait_ge(params, 16 * N_PARAMS)
                pe.wait_ge(ident_ready, 1)
                pe.transpose(prep_ps[0][:, 0:CR], fc1_in[:, :, :].rearrange("r a c -> r (a c)"), ident[0:CR, 0:CR])
                for g in range(7):
                    if g >= 2:
                        pe.wait_ge(prep_ev, g - 1)
                    for t in range(4 * g, min(4 * g + 4, K * K)):
                        mm = pe.transpose(prep_ps[1 + g % 2][0:CR, (t % 4) * P:(t % 4) * P + P], fc2_in[:, t, :], ident[:, :])
                    mm.then_inc(prep_mm, 1)
                pe.wait_ge(prep_ev, 1)
                for m in range(HALVES):
                    mm = pe.transpose(prep_ps[0][:, m * P:(m + 1) * P],
                                      expand_in[:, m, :, :].rearrange("o a c -> o (a c)"), ident[:, :])
                mm.then_inc(prep_mm, 1)
                for m in range(HALVES):
                    mm = pe.transpose(prep_ps[3][:, m * C:(m + 1) * C], shrink_in[:, m * P:(m + 1) * P], ident[0:C, 0:C])
                mm.then_inc(prep_mm, 1)
                pe.wait_ge(prep_ev, 9)
                for m in range(HALVES):
                    pe.matmul(prep_ps[0][:, m:m + 1], kept["expand_t"][:, m, 0, :], ln2[:, 1:2], start=True, stop=True)
                for hp in range(2):
                    for m in range(HALVES):
                        mm = pe.matmul(prep_ps[0][C * hp:C * hp + C, HALVES:HALVES + 1], kept["shrink_t"][:, m, :],
                                       beta_in[:, m:m + 1], start=(m == 0), stop=(m == HALVES - 1))
                mm.then_inc(prep_mm, 1)

            pe.wait_ge(line_zero, 1)
            pe.wait_ge(taps_ready, 1)
            prepare()
            run(pe, 0, step)
            pe.wait_ge(taps_ready, 4)
            run(pe, 1, step)
            pe.wait_ge(line_zero, 2)
            for s in (2, 3):
                run(pe, s, step)


def block_two(nc, bank, kept, out):
    by_h = kept["by_h"]
    conv_ps, stat_ps, wide_ps, exp_ps, out_ps = bank[0:2], bank[2], bank[3], bank[4:6], bank[6:8]
    with ExitStack() as ctx:
        def sb(name, shape, dt=F32):
            return ctx.enter_context(nc.sbuf_tensor(name, shape, dt))

        def sem(name):
            return ctx.enter_context(nc.semaphore(name))

        x_hi = sb("x_hi", [P, 2, XW, XJ], F32R)
        x_lo = sb("x_lo", [P, 2, XW, XJ], F32R)
        dyn_hi = sb("dyn_hi", [P, 2, KD * NE, 2, C], F32R)
        dyn_lo = sb("dyn_lo", [P, 2, KD * NE, 2, C], F32R)
        dyn_all = kept["dyn_all"]
        tap = sb("tap", [P, B, 2, KD * NE])
        tap_edge = sb("tap_edge", [P, 2, KD * NE])
        tap_all = sb("tap_all", [P, B, K * K])
        tap_now = sb("tap_now", [P, 2, K * K])
        inner = sb("inner", [P, 2, W, HP])
        swapped = sb("swapped", [P, W, HP + 1])
        centred = sb("centred", [P, PIX])
        squares = sb("squares", [P, PIX])
        normed = sb("normed", [P, COLS * 2])
        wide = sb("wide", [P, HALVES, 2, PIX])
        result = squares[:, :].rearrange("p (j w) -> p j w", w=W)
        hid = centred[0:LN1, 0:4 * CR].rearrange("b (n r) -> b n r", n=4)
        hst = centred[0:LN1, P:P + 4]
        hid_t = centred[0:CR, 2 * P:2 * P + B]
        pooled = centred[:, 3 * P:3 * P + B]
        std = kept["line_sum"][0:STAT_ROWS, :, :].rearrange("p b j -> p (b j)").rearrange(
            "p (a c) -> p a c", a=2)
        rstd_parts = kept["rstd_parts"]
        rstd_hi, rstd_lo = rstd_parts[0:STAT_ROWS, :], rstd_parts[STAT_ROWS:2 * STAT_ROWS, :]
        energy = sb("energy", [P, HALVES, 2, 2])
        resp = sb("resp", [P, 6, HALVES])
        shrink_now = kept["shrink_now"]
        eps_col = sb("eps_col", [P, 1])

        chain = sem("chain")
        CHAIN = 11
        eps_ready = sem("eps_ready")
        pool_mm = sem("pool_mm")
        pool_sd = sem("pool_sd")
        xhi_ready = sem("xhi_ready")
        xlo_ready = sem("xlo_ready")
        dyn_ready = sem("dyn_ready")
        edge_copied = sem("edge_copied")
        pads = sem("pads")
        swap_ready = sem("swap_ready")
        tap_copied = sem("tap_copied")
        inner_step = sem("inner_step")
        conv_done = sem("conv_done")
        conv_kept = sem("conv_kept")
        var_done = sem("var_done")
        std_ready = sem("std_ready")
        rstd_ready = sem("rstd_ready")
        wide_done = sem("wide_done")
        normed_ready = sem("normed_ready")
        exp_done = sem("exp_done")
        gelu_done = sem("gelu_done")
        energy_ready = sem("energy_ready")
        energy_sum = sem("energy_sum")
        resp_ready = sem("resp_ready")
        resp_mean = sem("resp_mean")
        shrink_ready = sem("shrink_ready")
        resp_step = sem("resp_step")
        rstd_step = sem("rstd_step")
        out_done = sem("out_done")
        result_ready = sem("result_ready")
        stored = sem("stored")

        def image(b):
            if isinstance(b, int):
                return by_h[:, b, :, :]
            return by_h[:, bass.ds(b, 1), :, :].rearrange("p a w j -> p (a w) j")

        inner_taps = ([(dh, dw) for dh in (0, -2, 2) for dw in (0, -1, 1)] +
                      [(dh, dw) for dh in (-1, 1) for dw in (0, -1, 1)])
        INNER = 2 * len(inner_taps)

        def batches(engine, step):
            step(0, 0, True)
            with engine.Fori(0, (B - 2) // 2) as i:
                for u in range(2):
                    step(1 + u + 2 * i, (1 + u) % 2, False)
            step(B - 1, (B - 1) % 2, False)

        block = ctx.enter_context(nc.Block())

        @block.sync
        def _(sp):
            o = out.rearrange("b c (j p) w -> b p c j w", p=2)
            for b in range(B):
                sp.wait_ge(result_ready, CHUNKS * (b + 1))
                for p in range(2):
                    sp.dma_start(o[b, p], result[C * p:C * p + C, :, :]).then_inc(stored, 16)
            sp.wait_ge(stored, 32 * B)

        @block.gpsimd
        def _(pool):
            def split_low(b, par):
                if not isinstance(b, int) or b >= 2:
                    pool.wait_ge(conv_done, CHUNKS * (b - 1))
                pool.wait_ge(xhi_ready, b + 1)
                pool.tensor_tensor(x_lo[:, par, 2:2 + W, 1:1 + HP], image(b),
                                  x_hi[:, par, 2:2 + W, 1:1 + HP].bitcast(F32), ALU.subtract).then_inc(xlo_ready, 1)

            def spread_taps(b, par):
                if not isinstance(b, int) or b > 0:
                    pool.wait_ge(dyn_ready, 2 * b)
                src = (tap[:, b, :, :] if isinstance(b, int) else
                       tap[:, bass.ds(b, 1), :, :].rearrange("p a o t -> p (a o) t"))
                pool.tensor_copy(tap_edge[:, :, :], src).then_inc(edge_copied, 1)
                pool.wait_ge(edge_copied, b + 1)
                if not isinstance(b, int) or b >= 2:
                    pool.wait_ge(conv_done, CHUNKS * (b - 1))
                shape = [P, KD * NE, 2, C]
                centre = kept["centre"][:, :].rearrange("p (a o c) -> p a o c", a=1, o=1).to_broadcast(shape)
                t = tap_edge[:, :, :].rearrange("p o (t a) -> p t o a", a=1).to_broadcast(shape)
                pool.tensor_tensor(dyn_hi[:, par, :, :, :], centre, t, ALU.mult)
                pool.tensor_tensor(dyn_all[:, :, :, :], centre, t, ALU.mult).then_inc(dyn_ready, 1)
                pool.wait_ge(dyn_ready, 2 * b + 1)
                pool.tensor_tensor(dyn_lo[:, par, :, :, :], dyn_all[:, :, :, :],
                                   dyn_hi[:, par, :, :, :].bitcast(F32), ALU.subtract).then_inc(dyn_ready, 1)

            def step(b, par):
                split_low(b, par)
                spread_taps(b, par)

            pool.wait_ge(pads, 1)
            pool.wait_ge(chain, CHAIN)
            spread_taps(0, 0)
            split_low(0, 0)
            with pool.Fori(0, (B - 2) // 2) as i:
                for u in range(2):
                    step(1 + u + 2 * i, (1 + u) % 2)
            step(B - 1, (B - 1) % 2)

        @block.scalar
        def _(act):
            def split_high(b, par):
                if not isinstance(b, int) or b >= 2:
                    act.wait_ge(conv_done, CHUNKS * (b - 1))
                act.activation(x_hi[:, par, 2:2 + W, 1:1 + HP], image(b), ACT.Copy).then_inc(xhi_ready, 1)

            def swap_rows(b):
                if not isinstance(b, int) or b > 0:
                    act.wait_ge(inner_step, INNER * b)
                for hp in range(2):
                    act.activation(swapped[C * hp:C * hp + C, :, 1 - hp:1 - hp + HP],
                                   image(b)[C * (1 - hp):C * (1 - hp) + C, :, :], ACT.Copy).then_inc(swap_ready, 1)

            act.wait_ge(pads, 1)
            split_high(0, 0)
            swap_rows(0)
            act.wait_ge(eps_ready, 1)
            act.wait_ge(chain, 5)
            act.activation(hst[:, 2:3], hst[:, 1:2], ACT.Sqrt, bias=eps_col[0:LN1, :], scale=1.0 / CR).then_inc(pool_sd, 1)

            def respond(b):
                act.wait_ge(energy_sum, b + 1)
                act.activation(resp[:, 1, :], resp[:, 0, :], ACT.Sqrt).then_inc(resp_ready, 1)

            def add_squares(b, n):
                half, m, hp = n // 4, n // 2 % 2, n % 2
                if n % 4 == 0:
                    act.wait_ge(gelu_done, 4 * CHUNKS * b + 2 * CHUNKS * (half + 1))
                    act.wait_ge(normed_ready, CHUNKS * b + 2 * (half + 1))
                else:
                    act.wait_ge(energy_ready, 8 * b + n)
                part = slice(half * PIX // 2, (half + 1) * PIX // 2)
                act.activation(centred[:, part], wide[:, m, hp, part], ACT.Square,
                               accum_out=energy[:, m, half, hp:hp + 1]).then_inc(energy_ready, 1)

            def step(b, par, is_first, last=False):
                if not is_first:
                    respond(b - 1)
                for q in range(CHUNKS):
                    act.wait_ge(conv_done, CHUNKS * b + q + 1)
                    if q == 0 and not is_first:
                        act.wait_ge(normed_ready, CHUNKS * b)
                        act.wait_ge(energy_ready, 8 * b)
                        act.wait_ge(var_done, b)
                    if q == 0 and (not isinstance(b, int) or b >= 2):
                        act.wait_ge(stored, 32 * (b - 1))
                    act.activation(centred[:, q * COLS:(q + 1) * COLS], conv_ps[q % 2][:, :], ACT.Copy)
                    act.activation(squares[:, q * COLS:(q + 1) * COLS], conv_ps[q % 2][:, :],
                                   ACT.Square).then_inc(conv_kept, 1)
                act.wait_ge(var_done, b + 1)
                act.activation(std[:, 0, :], stat_ps[0:STAT_ROWS, 0:STAT_COLS], ACT.Sqrt,
                               bias=eps_col[0:STAT_ROWS, :]).then_inc(std_ready, 1)
                if not last:
                    split_high(b + 1, 1 - par)
                    swap_rows(b + 1)
                for q in range(CHUNKS):
                    for hp in range(2):
                        for m in range(HALVES):
                            e = (q * 2 + hp) * HALVES + m
                            act.wait_ge(exp_done, 4 * CHUNKS * b + e + 1)
                            if e == 0 and not is_first:
                                act.wait_ge(out_done, CHUNKS * b)
                            act.activation(wide[:, m, hp, q * COLS:(q + 1) * COLS], exp_ps[e % 2][:, :],
                                           ACT.Gelu, bias=kept["expand_bias"][:, m:m + 1]).then_inc(gelu_done, 1)
                        if q >= 2:
                            add_squares(b, 2 * (q - 2) + hp)
                for n in range(4, 8):
                    add_squares(b, n)

            step(0, 0, True)
            with act.Fori(0, (B - 2) // 2) as i:
                for u in range(2):
                    step(1 + u + 2 * i, (1 + u) % 2, False)
            step(B - 1, (B - 1) % 2, False, True)
            respond(B - 1)

        @block.vector
        def _(dve):
            n_chain = [0]

            def link(ins):
                n_chain[0] += 1
                ins.then_inc(chain, 1)
                dve.wait_ge(chain, n_chain[0])

            dve.memset(eps_col[:, :], EPS).then_inc(eps_ready, 1)
            for t in (x_hi, x_lo):
                for w0 in (0, W + 2):
                    dve.memset(t[:, :, w0:w0 + 2, :].bitcast(F32), 0.0)
                for j in (0, HP + 1):
                    dve.memset(t[:, :, 2:2 + W, j:j + 1].bitcast(F32), 0.0)
            dve.memset(swapped[0:C, :, 0:1], 0.0)
            dve.memset(swapped[C:P, :, HP:HP + 1], 0.0).then_inc(pads, 1)
            dve.memset(tap[:, :, :, :].rearrange("p b o t -> p (b o t)"), 0.0)
            link(dve.tensor_reduce(pooled, kept["line_sum"][:, :, :], AX.X, ALU.add))
            dve.wait_ge(pool_mm, 1)
            link(dve.tensor_reduce(hst[:, 0:1], wide_ps[0:LN1, 0:CR], AX.X, ALU.add))
            link(dve.tensor_scalar(hst[:, 0:1], hst[:, 0:1], 1.0 / CR, None, ALU.mult))
            link(dve.tensor_scalar(hid[:, 0, :], wide_ps[0:LN1, 0:CR], hst[:, 0:1], None, ALU.subtract))
            link(dve.tensor_tensor_reduce(hid[:, 1, :], hid[:, 0, :], hid[:, 0, :], 1.0, 0.0, ALU.mult, ALU.add, hst[:, 1:2]))
            dve.wait_ge(pool_sd, 1)
            link(dve.reciprocal(hst[:, 3:4], hst[:, 2:3]))
            link(dve.scalar_tensor_tensor(out=hid[:, 2, :], in0=hid[:, 0, :], scalar=hst[:, 3:4],
                                          in1=kept["ln1_wb"][:, 0, :], op0=ALU.mult, op1=ALU.mult))
            link(dve.tensor_tensor(hid[:, 3, :], hid[:, 2, :], kept["ln1_wb"][:, 1, :], ALU.add))
            dve.wait_ge(pool_mm, 2)
            link(dve.tensor_copy(hid_t, wide_ps[0:CR, 0:B]))
            dve.wait_ge(pool_mm, 3)
            dve.tensor_copy(tap_all[:, :, :], stat_ps[:, 0:K * K * B].rearrange("p (t b) -> p b t", b=B))
            dyn = stat_ps[:, 0:K * K * B].rearrange("p (r s b) -> p b r s", r=K, s=K)
            t6 = tap[:, :, :, :].rearrange("p b o (d s) -> p b o d s", s=NE)
            for pi in range(2):
                for po in range(2):
                    r0 = pi - po
                    d0 = 1 if r0 < 0 else 0
                    for d in range(d0, d0 + KD - abs(r0)):
                        last = dve.tensor_copy(t6[C * pi:C * pi + C, :, po, d, :], dyn[C * pi:C * pi + C, :, r0 + 2 * d, 0:K:K - 1])
            link(last)
            for n in range(2):
                last = dve.tensor_copy(kept["spread"][STAT_ROWS * n:STAT_ROWS * (n + 1), :, :],
                                       kept["ident"][0:STAT_ROWS, 0:STAT_ROWS].rearrange("p (a o) -> p a o", o=1)
                                       .to_broadcast([STAT_ROWS, STAT_ROWS, C]))
            link(last)

            def load_taps(b, par):
                src = tap_all[:, b, :] if isinstance(b, int) else tap_all[:, bass.ds(b, 1), :].rearrange("p a t -> p (a t)")
                if not isinstance(b, int) or b >= 2:
                    dve.wait_ge(inner_step, INNER * (b - 1))
                dve.tensor_copy(tap_now[:, par, :], src).then_inc(tap_copied, 1)

            def take_taps(b, par, lo, hi):
                for m in range(lo, hi):
                    dh, dw = inner_taps[m // 2]
                    w0, w1 = (m % 2) * W // 2, (m % 2 + 1) * W // 2
                    w0, w1 = max(w0, -dw), min(w1, W - dw)
                    t = (dh + 2) * K + dw + 2
                    if dh % 2 == 0:
                        j0, j1 = max(0, -dh // 2), min(HP, HP - dh // 2)
                        src = image(b)[:, w0 + dw:w1 + dw, j0 + dh // 2:j1 + dh // 2]
                    else:
                        j0, j1 = 0, HP
                        src = swapped[:, w0 + dw:w1 + dw, (dh + 1) // 2:(dh + 1) // 2 + HP]
                    dst = inner[:, par, w0:w1, j0:j1]
                    if m == 0:
                        dve.wait_ge(tap_copied, b + 1)
                        if not isinstance(b, int) or b >= 2:
                            dve.wait_ge(conv_done, CHUNKS * (b - 1))
                    if dh % 2 and not inner_taps[m // 2 - 1][0] % 2 and m % 2 == 0:
                        dve.wait_ge(swap_ready, 2 * (b + 1))
                    if m < 2:
                        dve.tensor_scalar(dst, src, tap_now[:, par, t:t + 1], None, ALU.mult).then_inc(inner_step, 1)
                    else:
                        dve.wait_ge(inner_step, INNER * b + m - 1)
                        dve.scalar_tensor_tensor(out=dst, in0=src, scalar=tap_now[:, par, t:t + 1], in1=dst,
                                                 op0=ALU.mult, op1=ALU.add).then_inc(inner_step, 1)

            def sum_energy(b):
                dve.wait_ge(energy_ready, 8 * (b + 1))
                dve.tensor_reduce(resp[:, 0, :], energy[:, :, :, :].rearrange("p m a h -> p m (a h)"), AX.X,
                                  ALU.add).then_inc(energy_sum, 1)

            def respond(b):
                dve.wait_ge(resp_mean, b + 1)
                dve.tensor_scalar(resp[:, 2, 0:1], wide_ps[:, 0:1], EPS, None, ALU.add).then_inc(resp_step, 1)
                dve.wait_ge(resp_step, 4 * b + 1)
                dve.reciprocal(resp[:, 3, 0:1], resp[:, 2, 0:1]).then_inc(resp_step, 1)
                dve.wait_ge(resp_step, 4 * b + 2)
                dve.scalar_tensor_tensor(out=resp[:, 4, :], in0=resp[:, 1, :], scalar=resp[:, 3, 0:1],
                                         in1=kept["gamma"][:, :], op0=ALU.mult, op1=ALU.mult).then_inc(resp_step, 1)
                dve.wait_ge(resp_step, 4 * b + 3)
                dve.tensor_scalar(resp[:, 5, :], resp[:, 4, :], 1.0, None, ALU.add).then_inc(resp_step, 1)
                dve.wait_ge(resp_step, 4 * b + 4)
                for m in range(HALVES):
                    last = dve.tensor_scalar(shrink_now[:, m, :], kept["shrink_t"][:, m, :], resp[:, 5, m:m + 1],
                                             None, ALU.mult)
                last.then_inc(shrink_ready, 1)

            def finish(b, before=lambda q: None):
                for q in range(CHUNKS):
                    before(q)
                    dve.wait_ge(out_done, CHUNKS * b + q + 1)
                    dve.scalar_tensor_tensor(
                        out=result[:, :, q * CW:(q + 1) * CW].rearrange("p j w -> p w j"),
                        in0=out_ps[q % 2][:, :].rearrange("p (w j) -> p w j", w=CW),
                        scalar=kept["out_bias"][:, :], in1=image(b)[:, q * CW:(q + 1) * CW, :],
                        op0=ALU.add, op1=ALU.add).then_inc(result_ready, 1)

            BEFORE_ENERGY, BEFORE_RESPONSE, BEFORE_FINISH, BEFORE_NORMED, AFTER_NORMED = 5, 6, 1, 2, 2
            BEFORE_RSTD = (INNER - BEFORE_ENERGY - BEFORE_RESPONSE - CHUNKS * BEFORE_FINISH -
                           (CHUNKS - 1) * BEFORE_NORMED - AFTER_NORMED)

            def step(b, par, is_first, last=False):
                if not last:
                    load_taps(b + 1, 1 - par)

                def take(n):
                    if not last:
                        take_taps(b + 1, 1 - par, taken[0], taken[0] + n)
                    taken[0] += n

                taken = [0]
                take(BEFORE_ENERGY)
                if not is_first:
                    sum_energy(b - 1)
                take(BEFORE_RESPONSE)
                if not is_first:
                    respond(b - 1)
                take(BEFORE_RSTD)
                dve.wait_ge(std_ready, b + 1)
                dve.reciprocal(std[:, 1, :], std[:, 0, :]).then_inc(rstd_step, 1)
                dve.wait_ge(rstd_step, 2 * b + 1)
                dve.tensor_copy(rstd_hi, std[:, 1, :]).then_inc(rstd_step, 1)
                dve.wait_ge(rstd_step, 2 * b + 2)
                dve.tensor_tensor(rstd_lo, std[:, 1, :], rstd_hi.bitcast(F32),
                                  ALU.subtract).then_inc(rstd_ready, 1)
                if not is_first:
                    finish(b - 1, lambda q: take(BEFORE_FINISH))
                else:
                    take(CHUNKS * BEFORE_FINISH)
                for q in range(CHUNKS):
                    if q > 0:
                        take(BEFORE_NORMED)
                    dve.wait_ge(wide_done, CHUNKS * b + q + 1)
                    if q >= 2:
                        dve.wait_ge(exp_done, 4 * CHUNKS * b + 4 * (q - 1))
                    dve.tensor_tensor(normed[:, (q % 2) * COLS:(q % 2 + 1) * COLS],
                                      centred[:, q * COLS:(q + 1) * COLS], wide_ps[:, :],
                                      ALU.mult).then_inc(normed_ready, 1)
                take(AFTER_NORMED)

            load_taps(0, 0)
            take_taps(0, 0, 0, INNER)
            step(0, 0, True)
            with dve.Fori(0, (B - 2) // 2) as i:
                for u in range(2):
                    step(1 + u + 2 * i, (1 + u) % 2, False)
            step(B - 1, (B - 1) % 2, False, True)
            sum_energy(B - 1)
            respond(B - 1)
            dve.wait_ge(stored, 32 * (B - 1))
            finish(B - 1)

        @block.tensor
        def _(pe):
            pe.wait_ge(chain, 1)
            pe.matmul(wide_ps[0:LN1, 0:CR], pooled, kept["fc1_t"][:, :], start=True, stop=True).then_inc(pool_mm, 1)
            pe.wait_ge(chain, 8)
            pe.transpose(wide_ps[0:CR, 0:B], hid[:, 3, :], kept["ident"][0:LN1, 0:LN1]).then_inc(pool_mm, 1)
            pe.wait_ge(chain, 9)
            for t in range(K * K):
                mm = pe.matmul(stat_ps[:, t * B:(t + 1) * B], kept["fc2_t"][:, t, :], hid_t, start=True, stop=True)
            mm.then_inc(pool_mm, 1)

            def respond(b):
                pe.wait_ge(resp_ready, b + 1)
                for m in range(HALVES):
                    mm = pe.matmul(wide_ps[:, 0:1], kept["mean_ce"][:, :].to_broadcast([P, P]), resp[:, 1, m:m + 1],
                                   start=(m == 0), stop=(m == HALVES - 1))
                mm.then_inc(resp_mean, 1)

            def shrink(b):
                pe.wait_ge(shrink_ready, b + 1)
                for q in range(CHUNKS):
                    if q >= 2:
                        pe.wait_ge(result_ready, CHUNKS * b + q - 1)
                    for hp in range(2):
                        for m in range(HALVES):
                            mm = pe.matmul(out_ps[q % 2][C * hp:C * hp + C, :], shrink_now[:, m, :],
                                           wide[:, m, hp, q * COLS:(q + 1) * COLS],
                                           start=(m == 0), stop=(m == HALVES - 1))
                    mm.then_inc(out_done, 1)

            def step(b, par, is_first):
                pe.wait_ge(dyn_ready, 2 * b + 2)
                pe.wait_ge(xlo_ready, b + 1)
                for q in range(CHUNKS):
                    if not is_first or q >= 2:
                        pe.wait_ge(conv_kept, CHUNKS * b + q - 1)
                    n = 0
                    for d in range(KD):
                        for i, s in enumerate(EDGE):
                            t = d * NE + i
                            for w, v in ((dyn_hi, x_hi), (dyn_hi, x_lo), (dyn_lo, x_hi)):
                                pe.matmul(conv_ps[q % 2][:, :],
                                          w[:, par, t, :, :].rearrange("p o c -> p (o c)"),
                                          v[:, par, q * CW + s:(q + 1) * CW + s, d:d + HP],
                                          start=(n == 0), stop=False)
                                n += 1
                    pe.wait_ge(inner_step, INNER * b + INNER - 1 + q // 2)
                    mm = pe.matmul(conv_ps[q % 2][:, :], kept["centre_both"][:, :, :].rearrange("p o c -> p (o c)"),
                                   inner[:, par, q * CW:(q + 1) * CW, :].rearrange("p w j -> p (w j)"),
                                   start=False, stop=True)
                    mm.then_inc(conv_done, 1)
                    if q == 1 and not is_first:
                        respond(b - 1)
                pe.wait_ge(conv_kept, CHUNKS * (b + 1))
                for k in range(STATS):
                    mm = pe.matmul(stat_ps[0:STAT_ROWS, 0:STAT_COLS],
                                   kept["pick"][:, STAT_ROWS - 2 - 2 * k:2 * STAT_ROWS - 2 - 2 * k],
                                   squares[:, k * STAT_COLS:(k + 1) * STAT_COLS], start=(k == 0), stop=(k == STATS - 1))
                mm.then_inc(var_done, 1)
                if not is_first:
                    shrink(b - 1)
                pe.wait_ge(rstd_ready, b + 1)

                def widen(q):
                    if q > 0:
                        pe.wait_ge(normed_ready, CHUNKS * b + q)
                    for k in range(q * STATS // CHUNKS, (q + 1) * STATS // CHUNKS):
                        o = wide_ps[:, (k % 4) * STAT_COLS:(k % 4 + 1) * STAT_COLS]
                        w = kept["spread"][:, 2 * k:2 * k + 2, :].rearrange("p a c -> p (a c)")
                        mm = pe.matmul(o, w, rstd_parts[:, :], start=True, stop=True)
                    mm.then_inc(wide_done, 1)

                widen(0)
                for q in range(CHUNKS):
                    pe.wait_ge(normed_ready, CHUNKS * b + q + 1)
                    if q + 1 < CHUNKS:
                        widen(q + 1)
                    for hp in range(2):
                        for m in range(HALVES):
                            e = (q * 2 + hp) * HALVES + m
                            if not is_first or e >= 2:
                                pe.wait_ge(gelu_done, 4 * CHUNKS * b + e - 1)
                            pe.matmul(exp_ps[e % 2][:, :], kept["expand_t"][:, m, hp, :],
                                      normed[:, (q % 2) * COLS:(q % 2 + 1) * COLS],
                                      start=True, stop=True).then_inc(exp_done, 1)

            batches(pe, step)
            respond(B - 1)
            shrink(B - 1)


_INS = ['x', 'L0_conv_k_td', 'L0_conv_k_dt', 'L0_conv_k_lr', 'L0_conv_k_rl', 'L1_conv_w_fc1', 'L1_conv_ln1_w',
        'L1_conv_ln1_b', 'L1_conv_w_fc2', 'L1_conv_ln2_w', 'L1_conv_ln2_b', 'L1_conv_w_expand',
        'L1_conv_w_shrink', 'L1_conv_grn_gamma', 'L1_conv_grn_beta']
_OUT = ((8, 64, 64, 64), 'float32')


def kernel(**inputs):
    import numpy as _np
    import concourse.bacc as _bacc
    from concourse import mybir as _mybir
    from concourse.bass_utils import run_bass_kernel_spmd as _run

    nc = _bacc.Bacc("TRN2", target_bir_lowering=False, num_devices=1)
    arrays, args = {}, []
    for name in _INS:
        a = _np.ascontiguousarray(inputs[name])
        arrays[f"in_{name}_dram"] = a
        args.append(nc.dram_tensor(f"in_{name}_dram", a.shape, _mybir.dt.from_np(a.dtype), kind="ExternalInput").ap())
    shape, dtype = _OUT
    args.append(nc.dram_tensor("out_0_dram", shape, _mybir.dt.from_np(_np.dtype(dtype)), kind="ExternalOutput").ap())
    build(nc, *args)
    r = _run(nc, [arrays], core_ids=[0])
    return r.results[0]["out_0_dram"]
```

```python
import math
from contextlib import ExitStack

import concourse.bass as bass
from concourse import mybir

F32 = mybir.dt.float32
F32R = mybir.dt.float32r
ALU = mybir.AluOpType
ACT = mybir.ActivationFunctionType
AX = mybir.AxisListType

P = 128
B, C, H, W = 8, 64, 64, 64
TAPS = 9
REACH = 2
OFFSETS = 2 * REACH + 1
WP, HP = W // 2, H // 2
PADDED = WP + 2 * REACH
LINE = B * WP
UNROLL = 12
ROWS_A_LOAD = 4
SLOTS = 4
STAGES = 3
LOADS = H // ROWS_A_LOAD
BG = B // 2

K = 5
KD = 3
EDGE = (0, K - 1)
NE = len(EDGE)
CR, CE = C // 4, 4 * C
HALVES = CE // P
EPS = 1e-6
LN1 = 8
PIX = W * HP
CHUNKS = 4
CW = W // CHUNKS
COLS = PIX // CHUNKS
STAT_COLS = 256
STATS = PIX // STAT_COLS
STAT_ROWS = 2 * STATS
PART_ROWS = 32
XW, XJ = W + K - 1, HP + 2


def build(nc, x, k_td, k_dt, k_lr, k_rl, fc1, ln1_w, ln1_b, fc2, ln2_w, ln2_b,
          expand, shrink, gamma, beta, out):
    with ExitStack() as ctx:
        ctx.enter_context(nc.allow_non_contiguous_dma(reason="small parameters and rows of images"))
        bank = [ctx.enter_context(nc.psum_tensor(f"bank{i}", [P, 512], F32)) for i in range(8)]

        def sb(name, shape, dt=F32):
            return ctx.enter_context(nc.sbuf_tensor(name, shape, dt))

        kept = dict(
            by_h=sb("by_h", [P, B, W, HP]),
            ident=sb("ident", [P, P]),
            centre=sb("centre", [P, C]),
            centre_both=sb("centre_both", [P, 2, C]),
            line_sum=sb("line_sum", [P, B, HP]),
            pick=sb("pick", [P, 2 * STAT_ROWS - 2]),
            mean_ce=sb("mean_ce", [P, 1]),
            fc1_t=sb("fc1_t", [P, CR]),
            ln1_wb=sb("ln1_wb", [LN1, 2, CR]),
            expand_t=sb("expand_t", [P, HALVES, 2, P]),
            expand_bias=sb("expand_bias", [P, HALVES]),
            shrink_t=sb("shrink_t", [P, HALVES, C]),
            gamma=sb("gamma", [P, HALVES]),
            out_bias=sb("out_bias", [P, 1]),
        )
        later = (("dyn_all", [P, KD * NE, 2, C], F32),
                 ("spread", [2 * PART_ROWS, STAT_ROWS, C], F32R),
                 ("rstd_parts", [2 * PART_ROWS, STAT_COLS], F32R),
                 ("std", [STAT_ROWS, 2, STAT_COLS], F32),
                 ("shrink_now", [P, HALVES, C], F32))
        at = -(-nc.sbuf_base // 32) * 32
        sb("slab", [P, max(K * K * P, sum(math.prod(shape[1:]) for _, shape, _ in later))])
        kept["fc2_t"] = nc.alloc_sbuf_tensor_at("fc2_t", [CR, K * K, P], F32, offset=at)
        for name, shape, dt in later:
            kept[name] = nc.alloc_sbuf_tensor_at(name, shape, dt, offset=at)
            at += 4 * math.prod(shape[1:])
        scans(nc, bank, kept, x, (k_td, k_dt, k_lr, k_rl), fc1, ln1_w, ln1_b, fc2, ln2_w, ln2_b,
              expand, shrink, gamma, beta)
        block_two(nc, bank, kept, out)


def scans(nc, bank, kept, x, kernels, fc1, ln1_w, ln1_b, fc2, ln2_w, ln2_b,
          expand, shrink, gamma, beta):
    by_h, ident = kept["by_h"], kept["ident"]
    line_ps, prep_ps = bank[0:SLOTS], bank[SLOTS:8]
    with ExitStack() as ctx:
        def sb(name, shape, dt=F32):
            return ctx.enter_context(nc.sbuf_tensor(name, shape, dt))

        def sem(name):
            return ctx.enter_context(nc.semaphore(name))

        by_w = sb("by_w", [P, B, H, WP])
        stage = sb("stage", [P, STAGES, BG, ROWS_A_LOAD, W])
        taps = sb("taps", [P, 4, OFFSETS, 2, C])
        taps_hi = sb("taps_hi", [P, 4, OFFSETS, P], F32R)
        taps_lo = sb("taps_lo", [P, 4, OFFSETS, P], F32R)
        line_hi = sb("line_hi", [P, SLOTS, B, PADDED], F32R)
        line_lo = sb("line_lo", [P, SLOTS, B, PADDED], F32R)
        rest = sb("rest", [P, 2, LINE])
        fc1_in = sb("fc1_in", [CR, 2, C])
        fc2_in = sb("fc2_in", [P, K * K, CR])
        expand_in = sb("expand_in", [P, HALVES, 2, C])
        shrink_in = sb("shrink_in", [C, CE])
        ln2 = sb("ln2", [P, 2])
        beta_in = sb("beta_in", [P, HALVES])
        x_loaded = [sem(f"x_loaded{i}") for i in range(STAGES)]
        x_spread = sem("x_spread")
        taps_zero = sem("taps_zero")
        taps_loaded = [sem(f"taps_loaded{i}") for i in range(4)]
        taps_high = sem("taps_high")
        later_high = sem("later_high")
        taps_ready = sem("taps_ready")
        line_zero = sem("line_zero")
        main_done = sem("main_done")
        low_done = sem("low_done")
        high_ready = sem("high_ready")
        low_ready = sem("low_ready")
        rest_ready = sem("rest_ready")
        line_done = sem("line_done")
        summed = sem("summed")
        turned = sem("turned")
        params = sem("params")
        ident_zero = sem("ident_zero")
        ident_ready = sem("ident_ready")
        prep_mm = sem("prep_mm")
        prep_ev = sem("prep_ev")
        consts = sem("consts")
        centre_sum = sem("centre_sum")

        N_PARAMS = 15
        FC2_GROUPS = -(-K * K // 4)

        counts = [H, H - 1, W, W - 1]
        first = [sum(counts[:s]) for s in range(4)]

        def line(s, r):
            image = by_w if s < 2 else by_h
            if isinstance(r, int):
                return image[:, :, r, :]
            return image[:, :, bass.ds(r, 1), :].rearrange("p b a i -> p b (a i)")

        head = [n % UNROLL for n in counts]

        def run(engine, s, step):
            for k in range(head[s]):
                step(s, k, (first[s] + k) % SLOTS)
            with engine.Fori(0, counts[s] // UNROLL) as i:
                for u in range(UNROLL):
                    step(s, UNROLL * i + (head[s] + u), (first[s] + head[s] + u) % SLOTS)

        def line_of(s, k):
            return line(s, k if s % 2 == 0 else k * -1 + (counts[s] - 1))

        block = ctx.enter_context(nc.Block())

        @block.sync
        def _(sp):
            def load(n):
                for g in range(2):
                    sp.dma_start(
                        stage[C * g:C * g + C, n % STAGES, :, :, :].rearrange("c b h w -> c b (h w)"),
                        x[BG * g:BG * g + BG, :, ROWS_A_LOAD * n:ROWS_A_LOAD * (n + 1), :]
                        .rearrange("b c h w -> c b (h w)")).then_inc(x_loaded[n % STAGES], 16)

            def load_taps(s):
                k = kernels[s].rearrange("t i o -> i t o")
                for pi in range(2):
                    for po in range(2):
                        lo = pi - po
                        d0 = 1 if lo < 0 else 0
                        n = OFFSETS - abs(lo)
                        t0 = lo + 2 * d0
                        sp.dma_start(taps[C * pi:C * pi + C, s, d0:d0 + n, po, :],
                                     k[:, t0:t0 + 2 * n - 1:2, :]).then_inc(taps_loaded[s], 16)

            load(0)
            sp.wait_ge(taps_zero, 1)
            load_taps(0)
            load(1)
            load_taps(1)
            load(2)
            for s in range(2, 4):
                load_taps(s)
            sp.dma_start(fc1_in[:, 0, :], fc1).then_inc(params, 16)
            sp.dma_start(fc1_in[:, 1, :], fc1).then_inc(params, 16)
            for h in range(2):
                sp.dma_start(fc2_in[C * h:C * h + C, :, :],
                             fc2.rearrange("(c t) r -> c t r", t=K * K)).then_inc(params, 16)
                sp.dma_start(expand_in[:, :, h, :],
                             expand.rearrange("(m o) c -> o m c", m=HALVES)).then_inc(params, 16)
                sp.dma_start(ln2[C * h:C * h + C, 0:1],
                             ln2_w.rearrange("(c a) -> c a", a=1)).then_inc(params, 16)
                sp.dma_start(ln2[C * h:C * h + C, 1:2],
                             ln2_b.rearrange("(c a) -> c a", a=1)).then_inc(params, 16)
            sp.dma_start(shrink_in[:, :], shrink).then_inc(params, 16)
            sp.dma_start(kept["gamma"][:, :], gamma.rearrange("(m o) -> o m", m=HALVES)).then_inc(params, 16)
            sp.dma_start(beta_in[:, :], beta.rearrange("(m o) -> o m", m=HALVES)).then_inc(params, 16)
            for i, v in enumerate((ln1_w, ln1_b)):
                sp.dma_start(kept["ln1_wb"][:, i, :],
                             v.rearrange("(a r) -> a r", a=1).to_broadcast([LN1, CR])).then_inc(params, 16)
            for n in range(STAGES, LOADS):
                sp.wait_ge(x_spread, 4 * (n - STAGES + 1))
                load(n)

        @block.gpsimd
        def _(pool):
            pool.memset(ident[:, :], 0.0).then_inc(ident_zero, 1)
            pool.wait_ge(ident_zero, 1)
            pool.affine_select(out=ident[:, :], in_=ident[:, :], compare_op=ALU.not_equal, fill=1.0,
                               base=0, pattern=[[-1, P]], channel_multiplier=1).then_inc(ident_ready, 1)
            pool.memset(kept["pick"][:, :], 0.0)
            pool.memset(kept["mean_ce"][:, :], 1.0 / CE)
            pool.memset(kept["expand_t"][:, :, :, :], 0.0)
            pool.memset(kept["centre_both"][:, :, :], 0.0).then_inc(consts, 1)

            def step(s, k, slot):
                n = first[s] + k
                x_line = line_of(s, k)
                pool.wait_ge(high_ready, n + 1)
                pool.tensor_tensor(rest[:, slot % 2, :].rearrange("p (b i) -> p b i", b=B), x_line,
                                   line_hi[:, (slot + 1) % SLOTS, :, REACH:REACH + WP].bitcast(F32),
                                   ALU.subtract).then_inc(rest_ready, 1)

            def add_line(n, last_line):
                pool.wait_ge(line_done, n)
                pool.wait_ge(summed, n - first[3])
                pool.tensor_tensor(line_sum, line_sum, last_line, ALU.add).then_inc(summed, 1)

            def step_and_sum(s, k, slot):
                step(s, k, slot)
                if not isinstance(k, int) or k > 0:
                    add_line(first[s] + k, line(s, k * -1 + counts[s]))

            for s in range(3):
                run(pool, s, step)
            line_sum = kept["line_sum"][:, :, :]
            pool.wait_ge(line_done, first[3])
            pool.tensor_copy(line_sum, line(3, W - 1)).then_inc(summed, 1)
            run(pool, 3, step_and_sum)
            add_line(first[3] + counts[3], line(3, 0))

        @block.scalar
        def _(act):
            def spread(i, n, part):
                g, p, v = part // 2, part % 2, n % STAGES
                load = STAGES * i + n
                rows = (by_w[:, :, ROWS_A_LOAD * load:ROWS_A_LOAD * (load + 1), :] if isinstance(i, int) else
                        by_w[:, :, bass.ds(ROWS_A_LOAD * load, ROWS_A_LOAD), :])
                if part == 0:
                    act.wait_ge(x_loaded[v], 32 * i + 32 * (n // STAGES + 1))
                act.activation(
                    rows[C * p:C * p + C, BG * g:BG * g + BG, :, :].rearrange("c b h i -> c b (h i)"),
                    stage[C * g:C * g + C, v, :, :, :]
                    .rearrange("c b h (i p) -> c b (h i) p", p=2)[:, :, :, p],
                    ACT.Copy).then_inc(x_spread, 1)

            def turn(r, j, hp, count):
                if count is not None:
                    act.wait_ge(line_done, count)
                for p in range(2):
                    o = by_h[C * hp:C * hp + C, :, :, :].rearrange("c b (i p) j -> c b i p j", p=2)
                    if isinstance(j, int):
                        dst = o[:, :, :, p, j]
                    else:
                        dst = o[:, :, :, p, bass.ds(j, 1)].rearrange("c b i a -> c b (i a)")
                    src = (by_w[C * p:C * p + C, :, r, :] if isinstance(r, int) else
                           by_w[C * p:C * p + C, :, bass.ds(r, 1), :].rearrange("c b a i -> c b (a i)"))
                    act.activation(dst, src, ACT.Copy).then_inc(turned, 1)

            def split_taps(s):
                act.wait_ge(taps_loaded[s], 64)
                act.activation(taps_hi[:, s, :, :], taps[:, s, :, :, :].rearrange("p d o c -> p d (o c)"),
                               ACT.Copy).then_inc(later_high, 1)

            for n in range(STAGES):
                for part in range(4):
                    spread(0, n, part)
                if n > 0:
                    split_taps(n)
            split_taps(3)
            with act.Fori(1, LOADS // STAGES) as i:
                for n in range(STAGES):
                    for part in range(4):
                        spread(i, n, part)
            for part in range(4):
                spread(LOADS // STAGES, 0, part)

            def turn_line(i, u):
                turn(i * -UNROLL + (H - u), i * (-UNROLL // 2) + (H - u) // 2, (H - u) % 2,
                     first[1] + u - 1 + UNROLL * i)

            for u in range(1, head[1]):
                turn_line(0, u)
            with act.Fori(0, counts[1] // UNROLL) as i:
                for u in range(UNROLL):
                    turn_line(i, head[1] + u)
            turn(1, 0, 1, first[2] - 1)
            turn(0, 0, 0, first[2])

            act.wait_ge(prep_mm, 1)
            act.wait_ge(consts, 1)
            for hp in range(2):
                half = slice(C * hp, C * hp + C)
                ins = act.activation(kept["expand_t"][half, :, hp, :],
                                     prep_ps[0][half, 0:HALVES * P].rearrange("p (m o) -> p m o", m=HALVES), ACT.Copy)
            ins.then_inc(prep_ev, 1)
            act.wait_ge(prep_mm, 2)
            act.activation(kept["shrink_t"][:, :, :], prep_ps[1][:, 0:HALVES * C].rearrange("p (m c) -> p m c", m=HALVES),
                           ACT.Copy)
            act.activation(kept["fc1_t"][:, :], prep_ps[1][:, HALVES * C:HALVES * C + CR], ACT.Copy,
                           scale=1.0 / (H * W)).then_inc(prep_ev, 1)
            for g in range(FC2_GROUPS):
                n = min(4, K * K - 4 * g)
                act.wait_ge(prep_mm, 3 + g)
                act.activation(kept["fc2_t"][:, 4 * g:4 * g + n, :],
                               prep_ps[2 + g % 2][0:CR, 0:n * P].rearrange("r (t c) -> r t c", c=P),
                               ACT.Copy).then_inc(prep_ev, 1)

        @block.vector
        def _(dve):
            dve.memset(taps[0:C, :, 0, 1, :], 0.0)
            dve.memset(taps[C:P, :, OFFSETS - 1, 0, :], 0.0).then_inc(taps_zero, 1)
            for t in (line_hi, line_lo):
                dve.memset(t[:, 0, :, :].bitcast(F32), 0.0)
                for i0 in (0, REACH + WP):
                    last = dve.memset(t[:, 1:SLOTS, :, i0:i0 + REACH].bitcast(F32), 0.0)
            last.then_inc(line_zero, 1)

            def split_low(s):
                dve.tensor_tensor(taps_lo[:, s, :, :], taps[:, s, :, :, :].rearrange("p d o c -> p d (o c)"),
                                  taps_hi[:, s, :, :].bitcast(F32), ALU.subtract).then_inc(taps_ready, 1)

            def split_later(s):
                dve.wait_ge(later_high, s)
                split_low(s)

            dve.wait_ge(taps_loaded[0], 64)
            dve.tensor_copy(taps_hi[:, 0, :, :],
                            taps[:, 0, :, :, :].rearrange("p d o c -> p d (o c)")).then_inc(taps_high, 1)
            dve.wait_ge(taps_high, 1)
            split_low(0)

            def prepare_constants():
                dve.wait_ge(consts, 1)
                dve.memset(kept["pick"][0:C, STAT_ROWS - 2:STAT_ROWS - 1], 1.0 / C)
                dve.memset(kept["pick"][C:P, STAT_ROWS - 1:STAT_ROWS], 1.0 / C)
                dve.wait_ge(ident_ready, 1)
                dve.tensor_tensor(kept["centre"][:, :], ident[:, 0:C], ident[:, C:P], ALU.add).then_inc(centre_sum, 1)
                for hp in range(2):
                    half = slice(C * hp, C * hp + C)
                    dve.tensor_scalar(kept["centre_both"][half, hp, :], ident[half, half], 1.0 / C, None, ALU.subtract)
                dve.wait_ge(centre_sum, 1)
                dve.tensor_scalar(kept["centre"][:, :], kept["centre"][:, :], 1.0 / C, None, ALU.subtract)

            def prepare_biases():
                dve.wait_ge(prep_mm, 3 + FC2_GROUPS)
                dve.tensor_copy(kept["expand_bias"][:, :], prep_ps[0][:, 0:HALVES])
                dve.tensor_copy(kept["out_bias"][:, :], prep_ps[0][:, HALVES:HALVES + 1])
                dve.tensor_scalar(kept["expand_t"][:, :, :, :], kept["expand_t"][:, :, :, :], ln2[:, 0:1], None, ALU.mult)

            part = slice(REACH, REACH + WP)
            as_lines = lambda t: t.rearrange("p (b i) -> p b i", b=B)

            def keep_line(s, k, slot):
                made = (slot + 1) % SLOTS
                dve.wait_ge(low_ready, first[s] + k + 1)
                dve.tensor_tensor(line_of(s, k), line_hi[:, made, :, part].bitcast(F32),
                                  line_lo[:, made, :, part].bitcast(F32), ALU.add).then_inc(line_done, 1)

            def high(s, k, slot):
                n = first[s] + k
                x_line = line_of(s, k)
                dve.lower_ap(x_line)
                if not isinstance(n, int) or n >= SLOTS:
                    dve.wait_ge(line_done, n - SLOTS + 1)
                dve.wait_ge(main_done, n + 1)
                dve.scalar_tensor_tensor(out=line_hi[:, (slot + 1) % SLOTS, :, part],
                                         in0=as_lines(line_ps[slot][:, 0:LINE]), scalar=0.0,
                                         in1=x_line, op0=ALU.max, op1=ALU.add).then_inc(high_ready, 1)

            def low(s, k, slot):
                n = first[s] + k
                dve.wait_ge(rest_ready, n + 1)
                dve.wait_ge(low_done, n + 1)
                dve.scalar_tensor_tensor(out=line_lo[:, (slot + 1) % SLOTS, :, part],
                                         in0=as_lines(line_ps[slot][:, 0:LINE]), scalar=0.0,
                                         in1=as_lines(rest[:, slot % 2, :]), op0=ALU.max,
                                         op1=ALU.add).then_inc(low_ready, 1)

            def low_then_high(s, k, slot):
                low(s, k, slot)
                high(s, k + 2, (slot + 2) % SLOTS)
                keep_line(s, k, slot)

            def scan(s, meanwhile=()):
                for k in range(2):
                    high(s, k, (first[s] + k) % SLOTS)
                for k in range(head[s] - 2):
                    low_then_high(s, k, (first[s] + k) % SLOTS)
                for work in meanwhile:
                    work()
                with dve.Fori(0, counts[s] // UNROLL) as i:
                    for u in range(UNROLL):
                        if s == 0 and u % ROWS_A_LOAD == 0:
                            dve.wait_ge(x_spread, UNROLL * i + (head[0] + u + ROWS_A_LOAD))
                        low_then_high(s, UNROLL * i + (head[s] - 2 + u), (first[s] + head[s] - 2 + u) % SLOTS)
                for k in range(counts[s] - 2, counts[s]):
                    low(s, k, (first[s] + k) % SLOTS)
                    keep_line(s, k, (first[s] + k) % SLOTS)

            dve.wait_ge(x_spread, ROWS_A_LOAD)
            scan(0, [lambda: split_later(1)])
            scan(1, [lambda: split_later(2), prepare_constants])
            slot = first[2] % SLOTS
            dve.wait_ge(line_done, first[2])
            dve.memset(line_hi[:, slot, :, REACH:REACH + WP].bitcast(F32), 0.0)
            dve.memset(line_lo[:, slot, :, REACH:REACH + WP].bitcast(F32), 0.0).then_inc(line_zero, 1)
            dve.wait_ge(turned, 2 * H)
            scan(2, [lambda: split_later(3), prepare_biases])
            scan(3)

        @block.tensor
        def _(pe):
            def main_product(s, k, slot):
                n = first[s] + k
                if not isinstance(n, int) or n > 0:
                    pe.wait_ge(high_ready, n)
                for d in range(OFFSETS):
                    mm = pe.matmul(line_ps[slot][:, 0:LINE], taps_hi[:, s, d, :],
                                   line_hi[:, slot, :, d:d + WP], start=(d == 0), stop=(d == OFFSETS - 1))
                mm.then_inc(main_done, 1)

            def low_products(s, k, slot):
                n = first[s] + k
                for d in range(OFFSETS):
                    pe.matmul(line_ps[slot][:, 0:LINE], taps_lo[:, s, d, :],
                              line_hi[:, slot, :, d:d + WP], start=False, stop=False,
                              skip_group_check=True)
                if not isinstance(n, int) or n > 0:
                    pe.wait_ge(low_ready, n)
                for d in range(OFFSETS):
                    mm = pe.matmul(line_ps[slot][:, 0:LINE], taps_hi[:, s, d, :],
                                   line_lo[:, slot, :, d:d + WP], start=False, stop=(d == OFFSETS - 1),
                                   skip_group_check=True)
                mm.then_inc(low_done, 1)

            def step(s, k, slot):
                main_product(s, k + 1, (slot + 1) % SLOTS)
                low_products(s, k, slot)

            def scan(s):
                main_product(s, 0, first[s] % SLOTS)
                for k in range(head[s] - 1):
                    step(s, k, (first[s] + k) % SLOTS)
                with pe.Fori(0, counts[s] // UNROLL) as i:
                    for u in range(UNROLL):
                        step(s, UNROLL * i + (head[s] - 1 + u), (first[s] + head[s] - 1 + u) % SLOTS)
                pe.wait_ge(high_ready, first[s] + counts[s])
                low_products(s, counts[s] - 1, (first[s] + counts[s] - 1) % SLOTS)

            def prepare():
                pe.wait_ge(params, 16 * N_PARAMS)
                pe.wait_ge(ident_ready, 1)
                for m in range(HALVES):
                    mm = pe.transpose(prep_ps[0][:, m * P:(m + 1) * P],
                                      expand_in[:, m, :, :].rearrange("o a c -> o (a c)"), ident[:, :])
                mm.then_inc(prep_mm, 1)
                for m in range(HALVES):
                    pe.transpose(prep_ps[1][:, m * C:(m + 1) * C], shrink_in[:, m * P:(m + 1) * P], ident[0:C, 0:C])
                pe.transpose(prep_ps[1][:, HALVES * C:HALVES * C + CR], fc1_in[:, :, :].rearrange("r a c -> r (a c)"),
                             ident[0:CR, 0:CR]).then_inc(prep_mm, 1)
                for g in range(FC2_GROUPS):
                    if g >= 2:
                        pe.wait_ge(prep_ev, g + 1)
                    for t in range(4 * g, min(4 * g + 4, K * K)):
                        mm = pe.transpose(prep_ps[2 + g % 2][0:CR, (t % 4) * P:(t % 4) * P + P], fc2_in[:, t, :], ident[:, :])
                    mm.then_inc(prep_mm, 1)
                for m in range(HALVES):
                    pe.matmul(prep_ps[0][:, m:m + 1], kept["expand_t"][:, m, 0, :], ln2[:, 1:2], start=True, stop=True)
                for hp in range(2):
                    for m in range(HALVES):
                        mm = pe.matmul(prep_ps[0][C * hp:C * hp + C, HALVES:HALVES + 1], kept["shrink_t"][:, m, :],
                                       beta_in[:, m:m + 1], start=(m == 0), stop=(m == HALVES - 1))
                mm.then_inc(prep_mm, 1)

            pe.wait_ge(line_zero, 1)
            pe.wait_ge(taps_ready, 1)
            scan(0)
            pe.wait_ge(taps_ready, 2)
            scan(1)
            prepare()
            pe.wait_ge(taps_ready, 3)
            pe.wait_ge(line_zero, 2)
            scan(2)
            pe.wait_ge(taps_ready, 4)
            scan(3)


def block_two(nc, bank, kept, out):
    by_h = kept["by_h"]
    conv_ps, stat_ps, exp_ps, out_ps = bank[0:2], bank[2], bank[4:6], bank[6:8]
    wide_ps = (bank[3], stat_ps)
    with ExitStack() as ctx:
        def sb(name, shape, dt=F32):
            return ctx.enter_context(nc.sbuf_tensor(name, shape, dt))

        def sem(name):
            return ctx.enter_context(nc.semaphore(name))

        x_hi = sb("x_hi", [P, 2, XW, XJ], F32R)
        x_lo = sb("x_lo", [P, 2, XW, XJ], F32R)
        dyn_hi = sb("dyn_hi", [P, 2, KD * NE, 2, C], F32R)
        dyn_lo = sb("dyn_lo", [P, 2, KD * NE, 2, C], F32R)
        dyn_all = kept["dyn_all"]
        tap = sb("tap", [P, B, 2, KD * NE])
        tap_edge = sb("tap_edge", [P, 2, KD * NE])
        tap_inner = sb("tap_inner", [P, 2, KD * (K - NE)])
        tap_all = sb("tap_all", [P, B, K * K])
        tap_now = sb("tap_now", [P, 2, K * K])
        inner = sb("inner", [P, 2, W, HP])
        swapped = sb("swapped", [P, W, HP + 1])
        centred = sb("centred", [P, PIX])
        squares = sb("squares", [P, PIX])
        normed = sb("normed", [P, COLS * 2])
        at = -(-nc.sbuf_base // 32) * 32
        wide = sb("wide", [P, HALVES, 2, PIX])
        inner_bytes = 4 * KD * (K - NE) * P
        inner_hi, inner_lo, inner_all = (
            nc.alloc_sbuf_tensor_at(name, [P, KD * (K - NE), 2, C], dt, offset=at + n * inner_bytes)
            for n, (name, dt) in enumerate((("inner_hi", F32R), ("inner_lo", F32R), ("inner_all", F32))))
        result = squares[:, :].rearrange("p (j w) -> p j w", w=W)
        hid = centred[0:LN1, 0:4 * CR].rearrange("b (n r) -> b n r", n=4)
        hst = centred[0:LN1, P:P + 4]
        hid_t = centred[0:CR, 2 * P:2 * P + B]
        pooled = centred[:, 3 * P:3 * P + B]
        std = kept["std"]
        rstd_parts = kept["rstd_parts"]
        rstd_hi, rstd_lo = rstd_parts[0:STAT_ROWS, :], rstd_parts[PART_ROWS:PART_ROWS + STAT_ROWS, :]
        energy = sb("energy", [P, HALVES, 2, 2])
        resp = sb("resp", [P, 6, HALVES])
        shrink_now = kept["shrink_now"]
        eps_col = sb("eps_col", [P, 1])

        chain = sem("chain")
        EDGES_MADE, INNER_MADE = 10, 13
        eps_ready = sem("eps_ready")
        pool_mm = sem("pool_mm")
        pool_sd = sem("pool_sd")
        xhi_ready = sem("xhi_ready")
        xlo_ready = sem("xlo_ready")
        dyn_ready = sem("dyn_ready")
        edge_copied = sem("edge_copied")
        pads = sem("pads")
        swap_ready = sem("swap_ready")
        spread_ready = sem("spread_ready")
        tap_copied = sem("tap_copied")
        inner_step = sem("inner_step")
        conv_done = sem("conv_done")
        conv_kept = sem("conv_kept")
        var_done = sem("var_done")
        std_ready = sem("std_ready")
        rstd_ready = sem("rstd_ready")
        wide_done = sem("wide_done")
        normed_ready = sem("normed_ready")
        exp_done = sem("exp_done")
        gelu_done = sem("gelu_done")
        energy_ready = sem("energy_ready")
        energy_sum = sem("energy_sum")
        resp_ready = sem("resp_ready")
        resp_mean = sem("resp_mean")
        shrink_ready = sem("shrink_ready")
        resp_step = sem("resp_step")
        rstd_step = sem("rstd_step")
        out_done = sem("out_done")
        result_ready = sem("result_ready")
        stored = sem("stored")

        def image(b):
            if isinstance(b, int):
                return by_h[:, b, :, :]
            return by_h[:, bass.ds(b, 1), :, :].rearrange("p a w j -> p (a w) j")

        inner_taps = ([(dh, dw) for dh in (0, -2, 2) for dw in (0, -1, 1)] +
                      [(dh, dw) for dh in (-1, 1) for dw in (0, -1, 1)])
        INNER = 2 * len(inner_taps)

        def batches(engine, step):
            step(0, 0, True)
            with engine.Fori(0, (B - 2) // 2) as i:
                for u in range(2):
                    step(1 + u + 2 * i, (1 + u) % 2, False)
            step(B - 1, (B - 1) % 2, False)

        block = ctx.enter_context(nc.Block())

        @block.sync
        def _(sp):
            o = out.rearrange("b c (j p) w -> b p c j w", p=2)
            for b in range(B):
                sp.wait_ge(result_ready, CHUNKS * (b + 1))
                for p in range(2):
                    sp.dma_start(o[b, p], result[C * p:C * p + C, :, :]).then_inc(stored, 16)
            sp.wait_ge(stored, 32 * B)

        @block.gpsimd
        def _(pool):
            def split_low(b, par):
                if not isinstance(b, int) or b >= 2:
                    pool.wait_ge(conv_done, CHUNKS * (b - 1))
                pool.wait_ge(xhi_ready, b + 1)
                pool.tensor_tensor(x_lo[:, par, 2:2 + W, 1:1 + HP], image(b),
                                  x_hi[:, par, 2:2 + W, 1:1 + HP].bitcast(F32), ALU.subtract).then_inc(xlo_ready, 1)

            def spread_taps(b, par):
                if not isinstance(b, int) or b > 0:
                    pool.wait_ge(dyn_ready, 2 * b)
                src = (tap[:, b, :, :] if isinstance(b, int) else
                       tap[:, bass.ds(b, 1), :, :].rearrange("p a o t -> p (a o) t"))
                pool.tensor_copy(tap_edge[:, :, :], src).then_inc(edge_copied, 1)
                pool.wait_ge(edge_copied, b + 1)
                if not isinstance(b, int) or b >= 2:
                    pool.wait_ge(conv_done, CHUNKS * (b - 1))
                shape = [P, KD * NE, 2, C]
                centre = kept["centre"][:, :].rearrange("p (a o c) -> p a o c", a=1, o=1).to_broadcast(shape)
                t = tap_edge[:, :, :].rearrange("p o (t a) -> p t o a", a=1).to_broadcast(shape)
                pool.tensor_tensor(dyn_hi[:, par, :, :, :], centre, t, ALU.mult)
                pool.tensor_tensor(dyn_all[:, :, :, :], centre, t, ALU.mult).then_inc(dyn_ready, 1)
                pool.wait_ge(dyn_ready, 2 * b + 1)
                pool.tensor_tensor(dyn_lo[:, par, :, :, :], dyn_all[:, :, :, :],
                                   dyn_hi[:, par, :, :, :].bitcast(F32), ALU.subtract).then_inc(dyn_ready, 1)

            def step(b, par):
                split_low(b, par)
                spread_taps(b, par)

            pool.wait_ge(pads, 1)
            pool.wait_ge(chain, EDGES_MADE)
            spread_taps(0, 0)
            with pool.Fori(0, (B - 2) // 2) as i:
                for u in range(2):
                    step(1 + u + 2 * i, (1 + u) % 2)
            step(B - 1, (B - 1) % 2)

        @block.scalar
        def _(act):
            def split_high(b, par):
                act.activation(x_hi[:, par, 2:2 + W, 1:1 + HP], image(b), ACT.Copy).then_inc(xhi_ready, 1)

            def swap_rows(b, hp):
                if hp == 0 and (not isinstance(b, int) or b > 1):
                    act.wait_ge(inner_step, INNER * (b - 1))
                act.activation(swapped[C * hp:C * hp + C, :, 1 - hp:1 - hp + HP],
                               image(b)[C * (1 - hp):C * (1 - hp) + C, :, :], ACT.Copy).then_inc(swap_ready, 1)

            act.wait_ge(eps_ready, 1)
            act.wait_ge(chain, 5)
            act.activation(hst[:, 2:3], hst[:, 1:2], ACT.Sqrt, bias=eps_col[0:LN1, :], scale=1.0 / CR).then_inc(pool_sd, 1)
            act.wait_ge(pads, 1)
            split_high(0, 0)
            for hp in range(2):
                swap_rows(1, hp)
            act.wait_ge(pool_mm, 3)
            for n in range(2):
                last = act.activation(kept["spread"][PART_ROWS * n:PART_ROWS * (n + 1), :, :],
                                      kept["ident"][0:PART_ROWS, 0:STAT_ROWS].rearrange("p (a o) -> p a o", o=1)
                                      .to_broadcast([PART_ROWS, STAT_ROWS, C]), ACT.Copy)
            last.then_inc(spread_ready, 1)

            def respond(b):
                act.wait_ge(energy_sum, b + 1)
                act.activation(resp[:, 1, :], resp[:, 0, :], ACT.Sqrt).then_inc(resp_ready, 1)

            def add_squares(b, n):
                half, m, hp = n // 4, n // 2 % 2, n % 2
                if n % 4 == 0:
                    act.wait_ge(gelu_done, 4 * CHUNKS * b + 2 * CHUNKS * (half + 1))
                    act.wait_ge(normed_ready, CHUNKS * b + 2 * (half + 1))
                else:
                    act.wait_ge(energy_ready, 8 * b + n)
                part = slice(half * PIX // 2, (half + 1) * PIX // 2)
                act.activation(centred[:, part], wide[:, m, hp, part], ACT.Square,
                               accum_out=energy[:, m, half, hp:hp + 1]).then_inc(energy_ready, 1)

            def step(b, par, is_first, last=False):
                for q in range(CHUNKS):
                    act.wait_ge(conv_done, CHUNKS * b + q + 1)
                    if q == 0 and not is_first:
                        act.wait_ge(normed_ready, CHUNKS * b)
                        act.wait_ge(energy_ready, 8 * b)
                        act.wait_ge(var_done, b)
                    if q == 0 and (not isinstance(b, int) or b >= 2):
                        act.wait_ge(stored, 32 * (b - 1))
                    act.activation(centred[:, q * COLS:(q + 1) * COLS], conv_ps[q % 2][:, :], ACT.Copy)
                    act.activation(squares[:, q * COLS:(q + 1) * COLS], conv_ps[q % 2][:, :],
                                   ACT.Square).then_inc(conv_kept, 1)
                    if q == 1 and not is_first:
                        respond(b - 1)
                    if q in (1, 2) and not is_first and not last:
                        swap_rows(b + 1, q - 1)
                act.wait_ge(var_done, b + 1)
                act.activation(std[:, 0, :], stat_ps[0:STAT_ROWS, 0:STAT_COLS], ACT.Sqrt,
                               bias=eps_col[0:STAT_ROWS, :]).then_inc(std_ready, 1)
                if not last:
                    split_high(b + 1, 1 - par)
                for q in range(CHUNKS):
                    for hp in range(2):
                        for m in range(HALVES):
                            e = (q * 2 + hp) * HALVES + m
                            act.wait_ge(exp_done, 4 * CHUNKS * b + e + 1)
                            if e == 0 and not is_first:
                                act.wait_ge(out_done, CHUNKS * b)
                            act.activation(wide[:, m, hp, q * COLS:(q + 1) * COLS], exp_ps[e % 2][:, :],
                                           ACT.Gelu, bias=kept["expand_bias"][:, m:m + 1]).then_inc(gelu_done, 1)
                        if q == CHUNKS - 1:
                            add_squares(b, hp)
                for n in range(2, 8):
                    add_squares(b, n)

            step(0, 0, True)
            with act.Fori(0, (B - 2) // 2) as i:
                for u in range(2):
                    step(1 + u + 2 * i, (1 + u) % 2, False)
            step(B - 1, (B - 1) % 2, False, True)
            respond(B - 1)

        @block.vector
        def _(dve):
            n_chain = [0]

            def link(ins):
                n_chain[0] += 1
                ins.then_inc(chain, 1)
                dve.wait_ge(chain, n_chain[0])

            dve.memset(eps_col[:, :], EPS).then_inc(eps_ready, 1)
            for t in (x_hi, x_lo):
                for w0 in (0, W + 2):
                    dve.memset(t[:, :, w0:w0 + 2, :].bitcast(F32), 0.0)
                for j in (0, HP + 1):
                    dve.memset(t[:, :, 2:2 + W, j:j + 1].bitcast(F32), 0.0)
            dve.memset(swapped[0:C, :, 0:1], 0.0)
            dve.memset(swapped[C:P, :, HP:HP + 1], 0.0).then_inc(pads, 1)
            dve.memset(tap[:, :, :, :].rearrange("p b o t -> p (b o t)"), 0.0)
            dve.memset(tap_inner[:, :, :].rearrange("p o t -> p (o t)"), 0.0)
            link(dve.tensor_reduce(pooled, kept["line_sum"][:, :, :], AX.X, ALU.add))
            dve.wait_ge(pool_mm, 1)
            link(dve.tensor_reduce(hst[:, 0:1], wide_ps[0][0:LN1, 0:CR], AX.X, ALU.add))
            link(dve.tensor_scalar(hst[:, 0:1], hst[:, 0:1], 1.0 / CR, None, ALU.mult))
            link(dve.tensor_scalar(hid[:, 0, :], wide_ps[0][0:LN1, 0:CR], hst[:, 0:1], None, ALU.subtract))
            link(dve.tensor_tensor_reduce(hid[:, 1, :], hid[:, 0, :], hid[:, 0, :], 1.0, 0.0, ALU.mult, ALU.add, hst[:, 1:2]))
            dve.wait_ge(pool_sd, 1)
            link(dve.reciprocal(hst[:, 3:4], hst[:, 2:3]))
            link(dve.scalar_tensor_tensor(out=hid[:, 2, :], in0=hid[:, 0, :], scalar=hst[:, 3:4],
                                          in1=kept["ln1_wb"][:, 0, :], op0=ALU.mult, op1=ALU.mult))
            link(dve.tensor_tensor(hid[:, 3, :], hid[:, 2, :], kept["ln1_wb"][:, 1, :], ALU.add))
            dve.wait_ge(pool_mm, 2)
            link(dve.tensor_copy(hid_t, wide_ps[0][0:CR, 0:B]))
            dve.wait_ge(xhi_ready, 1)
            dve.tensor_tensor(x_lo[:, 0, 2:2 + W, 1:1 + HP], image(0),
                              x_hi[:, 0, 2:2 + W, 1:1 + HP].bitcast(F32), ALU.subtract).then_inc(xlo_ready, 1)
            dve.wait_ge(pool_mm, 3)
            dve.tensor_copy(tap_all[:, :, :], stat_ps[:, 0:K * K * B].rearrange("p (t b) -> p b t", b=B))
            dyn = stat_ps[:, 0:K * K * B].rearrange("p (r s b) -> p b r s", r=K, s=K)
            t6 = tap[:, :, :, :].rearrange("p b o (d s) -> p b o d s", s=NE)
            for pi in range(2):
                for po in range(2):
                    r0 = pi - po
                    d0 = 1 if r0 < 0 else 0
                    for d in range(d0, d0 + KD - abs(r0)):
                        last = dve.tensor_copy(t6[C * pi:C * pi + C, :, po, d, :], dyn[C * pi:C * pi + C, :, r0 + 2 * d, 0:K:K - 1])
            link(last)
            dve.memset(rstd_parts[:, :].bitcast(F32), 0.0)
            t3 = tap_inner[:, :, :].rearrange("p o (d s) -> p o d s", s=K - NE)
            for pi in range(2):
                for po in range(2):
                    r0 = pi - po
                    d0 = 1 if r0 < 0 else 0
                    for d in range(d0, d0 + KD - abs(r0)):
                        last = dve.tensor_copy(t3[C * pi:C * pi + C, po, d, :], dyn[C * pi:C * pi + C, 0, r0 + 2 * d, 1:K - 1])
            link(last)
            shape = [P, KD * (K - NE), 2, C]
            centre = kept["centre"][:, :].rearrange("p (a o c) -> p a o c", a=1, o=1).to_broadcast(shape)
            t = tap_inner[:, :, :].rearrange("p o (t a) -> p t o a", a=1).to_broadcast(shape)
            dve.tensor_tensor(inner_hi[:, :, :, :], centre, t, ALU.mult)
            link(dve.tensor_tensor(inner_all[:, :, :, :], centre, t, ALU.mult))
            link(dve.tensor_tensor(inner_lo[:, :, :, :], inner_all[:, :, :, :],
                                   inner_hi[:, :, :, :].bitcast(F32), ALU.subtract))


            def load_taps(b, par):
                src = tap_all[:, b, :] if isinstance(b, int) else tap_all[:, bass.ds(b, 1), :].rearrange("p a t -> p (a t)")
                dve.tensor_copy(tap_now[:, par, :], src).then_inc(tap_copied, 1)

            def take_taps(b, par, lo, hi):
                for m in range(lo, hi):
                    n, half = m // 2, m % 2
                    dh, dw = inner_taps[n]
                    w0, w1 = max(half * W // 2, -dw), min((half + 1) * W // 2, W - dw)
                    if dh % 2 == 0:
                        j0, j1 = max(0, -dh // 2), min(HP, HP - dh // 2)
                        src = image(b)[:, w0 + dw:w1 + dw, j0 + dh // 2:j1 + dh // 2]
                    else:
                        j0, j1 = 0, HP
                        src = swapped[:, w0 + dw:w1 + dw, (dh + 1) // 2:(dh + 1) // 2 + HP]
                    dst = inner[:, par, w0:w1, j0:j1]
                    t = (dh + 2) * K + dw + 2
                    if m == 0:
                        dve.wait_ge(tap_copied, b)
                        if not isinstance(b, int) or b >= 2:
                            dve.wait_ge(conv_done, CHUNKS * (b - 1))
                    if half == 0 and dh % 2 and inner_taps[n - 1][0] % 2 == 0:
                        dve.wait_ge(swap_ready, 2 * b)
                    if n == 0:
                        dve.tensor_scalar(dst, src, tap_now[:, par, t:t + 1], None, ALU.mult).then_inc(inner_step, 1)
                    else:
                        dve.wait_ge(inner_step, INNER * (b - 1) + m - 1)
                        dve.scalar_tensor_tensor(out=dst, in0=src, scalar=tap_now[:, par, t:t + 1], in1=dst,
                                                 op0=ALU.mult, op1=ALU.add).then_inc(inner_step, 1)

            def sum_energy(b):
                dve.wait_ge(energy_ready, 8 * (b + 1))
                dve.tensor_reduce(resp[:, 0, :], energy[:, :, :, :].rearrange("p m a h -> p m (a h)"), AX.X,
                                  ALU.add).then_inc(energy_sum, 1)

            def respond(b):
                dve.wait_ge(resp_mean, b + 1)
                dve.tensor_scalar(resp[:, 2, 0:1], wide_ps[0][:, 0:1], EPS, None, ALU.add).then_inc(resp_step, 1)
                dve.wait_ge(resp_step, 4 * b + 1)
                dve.reciprocal(resp[:, 3, 0:1], resp[:, 2, 0:1]).then_inc(resp_step, 1)
                dve.wait_ge(resp_step, 4 * b + 2)
                dve.scalar_tensor_tensor(out=resp[:, 4, :], in0=resp[:, 1, :], scalar=resp[:, 3, 0:1],
                                         in1=kept["gamma"][:, :], op0=ALU.mult, op1=ALU.mult).then_inc(resp_step, 1)
                dve.wait_ge(resp_step, 4 * b + 3)
                dve.tensor_scalar(resp[:, 5, :], resp[:, 4, :], 1.0, None, ALU.add).then_inc(resp_step, 1)
                dve.wait_ge(resp_step, 4 * b + 4)
                for m in range(HALVES):
                    last = dve.tensor_scalar(shrink_now[:, m, :], kept["shrink_t"][:, m, :], resp[:, 5, m:m + 1],
                                             None, ALU.mult)
                last.then_inc(shrink_ready, 1)

            def finish(b, q):
                dve.wait_ge(out_done, CHUNKS * b + q + 1)
                dve.scalar_tensor_tensor(
                    out=result[:, :, q * CW:(q + 1) * CW].rearrange("p j w -> p w j"),
                    in0=out_ps[q % 2][:, :].rearrange("p (w j) -> p w j", w=CW),
                    scalar=kept["out_bias"][:, :], in1=image(b)[:, q * CW:(q + 1) * CW, :],
                    op0=ALU.add, op1=ALU.add).then_inc(result_ready, 1)

            BEFORE_ENERGY, BEFORE_RESPONSE, BEFORE_FINISH, BEFORE_NORMED, AFTER_NORMED = 8, 8, 2, 2, 3
            BEFORE_RSTD = (INNER - BEFORE_ENERGY - BEFORE_RESPONSE - 2 * BEFORE_FINISH -
                           2 * BEFORE_NORMED - AFTER_NORMED)

            def step(b, par, is_first, last=False):
                if not last:
                    load_taps(b + 1, 1 - par)

                def take(n):
                    if not last:
                        take_taps(b + 1, 1 - par, taken[0], min(taken[0] + n, INNER))
                    taken[0] += n

                taken = [0]
                if is_first:
                    take(INNER - taken[0])
                take(BEFORE_ENERGY)
                if not is_first:
                    sum_energy(b - 1)
                take(BEFORE_RESPONSE)
                if not is_first:
                    respond(b - 1)
                take(BEFORE_RSTD)
                if not is_first:
                    dve.wait_ge(var_done, b + 1)
                    finish(b - 1, 0)
                dve.wait_ge(std_ready, b + 1)
                dve.reciprocal(std[:, 1, :], std[:, 0, :]).then_inc(rstd_step, 1)
                dve.wait_ge(rstd_step, 2 * b + 1)
                dve.tensor_copy(rstd_hi, std[:, 1, :]).then_inc(rstd_step, 1)
                dve.wait_ge(rstd_step, 2 * b + 2)
                dve.tensor_tensor(rstd_lo, std[:, 1, :], rstd_hi.bitcast(F32),
                                  ALU.subtract).then_inc(rstd_ready, 1)
                def norm(q):
                    dve.wait_ge(wide_done, CHUNKS * b + q + 1)
                    if q >= 2:
                        dve.wait_ge(exp_done, 4 * CHUNKS * b + 4 * (q - 1))
                    dve.tensor_tensor(normed[:, (q % 2) * COLS:(q % 2 + 1) * COLS],
                                      centred[:, q * COLS:(q + 1) * COLS], wide_ps[q % 2][:, :],
                                      ALU.mult).then_inc(normed_ready, 1)

                if not is_first:
                    finish(b - 1, 1)
                norm(0)
                take(BEFORE_FINISH)
                if not is_first:
                    finish(b - 1, 2)
                norm(1)
                take(BEFORE_FINISH)
                if not is_first:
                    finish(b - 1, 3)
                for q in range(2, CHUNKS):
                    take(BEFORE_NORMED)
                    norm(q)
                take(AFTER_NORMED)

            step(0, 0, True)
            with dve.Fori(0, (B - 2) // 2) as i:
                for u in range(2):
                    step(1 + u + 2 * i, (1 + u) % 2, False)
            step(B - 1, (B - 1) % 2, False, True)
            sum_energy(B - 1)
            respond(B - 1)
            dve.wait_ge(stored, 32 * (B - 1))
            for q in range(CHUNKS):
                finish(B - 1, q)

        @block.tensor
        def _(pe):
            pe.wait_ge(chain, 1)
            pe.matmul(wide_ps[0][0:LN1, 0:CR], pooled, kept["fc1_t"][:, :], start=True, stop=True).then_inc(pool_mm, 1)
            pe.wait_ge(chain, 8)
            pe.transpose(wide_ps[0][0:CR, 0:B], hid[:, 3, :], kept["ident"][0:LN1, 0:LN1]).then_inc(pool_mm, 1)
            pe.wait_ge(chain, 9)
            for t in range(K * K):
                mm = pe.matmul(stat_ps[:, t * B:(t + 1) * B], kept["fc2_t"][:, t, :], hid_t, start=True, stop=True)
            mm.then_inc(pool_mm, 1)

            def respond(b):
                pe.wait_ge(resp_ready, b + 1)
                for m in range(HALVES):
                    mm = pe.matmul(wide_ps[0][:, 0:1], kept["mean_ce"][:, :].to_broadcast([P, P]), resp[:, 1, m:m + 1],
                                   start=(m == 0), stop=(m == HALVES - 1))
                mm.then_inc(resp_mean, 1)

            def variance(b, q):
                pe.wait_ge(conv_kept, CHUNKS * b + q + 1)
                for k in range(q * STATS // CHUNKS, (q + 1) * STATS // CHUNKS):
                    mm = pe.matmul(stat_ps[0:STAT_ROWS, 0:STAT_COLS],
                                   kept["pick"][:, STAT_ROWS - 2 - 2 * k:2 * STAT_ROWS - 2 - 2 * k],
                                   squares[:, k * STAT_COLS:(k + 1) * STAT_COLS], start=(k == 0), stop=(k == STATS - 1))
                if q == CHUNKS - 1:
                    mm.then_inc(var_done, 1)

            def shrink(b, q):
                if q == 0:
                    pe.wait_ge(shrink_ready, b + 1)
                if q >= 2:
                    pe.wait_ge(result_ready, CHUNKS * b + q - 1)
                for hp in range(2):
                    for m in range(HALVES):
                        mm = pe.matmul(out_ps[q % 2][C * hp:C * hp + C, :], shrink_now[:, m, :],
                                       wide[:, m, hp, q * COLS:(q + 1) * COLS],
                                       start=(m == 0), stop=(m == HALVES - 1))
                mm.then_inc(out_done, 1)

            def step(b, par, is_first):
                pe.wait_ge(dyn_ready, 2 * b + 2)
                pe.wait_ge(xlo_ready, b + 1)
                for q in range(CHUNKS):
                    if not is_first or q >= 2:
                        pe.wait_ge(conv_kept, CHUNKS * b + q - 1)
                    columns = [(dyn_hi[:, par], dyn_lo[:, par], NE, EDGE)]
                    if is_first:
                        columns.append((inner_hi[:, :], inner_lo[:, :], K - NE, range(1, K - 1)))
                    n = 0
                    for hi, lo, ns, ss in columns:
                        if n > 0 and q == 0:
                            pe.wait_ge(chain, INNER_MADE)
                        for d in range(KD):
                            for i, s in enumerate(ss):
                                for w, v in ((hi, x_hi), (hi, x_lo), (lo, x_hi)):
                                    n += 1
                                    mm = pe.matmul(conv_ps[q % 2][:, :],
                                                   w[:, d * ns + i, :, :].rearrange("p o c -> p (o c)"),
                                                   v[:, par, q * CW + s:(q + 1) * CW + s, d:d + HP],
                                                   start=(n == 1), stop=(is_first and n == 3 * KD * K))
                    if not is_first:
                        pe.wait_ge(inner_step, INNER * (b - 1) + INNER - 1 + q // 2)
                        mm = pe.matmul(conv_ps[q % 2][:, :], kept["centre_both"][:, :, :].rearrange("p o c -> p (o c)"),
                                       inner[:, par, q * CW:(q + 1) * CW, :].rearrange("p w j -> p (w j)"),
                                       start=False, stop=True)
                    mm.then_inc(conv_done, 1)
                    if q == 2 and not is_first:
                        respond(b - 1)
                    if q > 0:
                        variance(b, q - 1)
                if not is_first:
                    shrink(b - 1, 0)
                variance(b, CHUNKS - 1)
                if not is_first:
                    for q in range(1, CHUNKS - 1):
                        shrink(b - 1, q)
                pe.wait_ge(rstd_ready, b + 1)

                def widen(q):
                    if q >= 2:
                        pe.wait_ge(normed_ready, CHUNKS * b + q - 1)
                    for k in range(q * STATS // CHUNKS, (q + 1) * STATS // CHUNKS):
                        o = wide_ps[q % 2][:, (k % (COLS // STAT_COLS)) * STAT_COLS:
                                           (k % (COLS // STAT_COLS) + 1) * STAT_COLS]
                        w = kept["spread"][:, 2 * k:2 * k + 2, :].rearrange("p a c -> p (a c)")
                        mm = pe.matmul(o, w, rstd_parts[:, :], start=True, stop=True)
                    mm.then_inc(wide_done, 1)

                if is_first:
                    pe.wait_ge(spread_ready, 1)
                widen(0)
                widen(1)
                if not is_first:
                    shrink(b - 1, CHUNKS - 1)
                for q in range(CHUNKS):
                    pe.wait_ge(normed_ready, CHUNKS * b + q + 1)
                    for hp in range(2):
                        for m in range(HALVES):
                            e = (q * 2 + hp) * HALVES + m
                            if not is_first or e >= 2:
                                pe.wait_ge(gelu_done, 4 * CHUNKS * b + e - 1)
                            pe.matmul(exp_ps[e % 2][:, :], kept["expand_t"][:, m, hp, :],
                                      normed[:, (q % 2) * COLS:(q % 2 + 1) * COLS],
                                      start=True, stop=True).then_inc(exp_done, 1)
                    if q + 2 < CHUNKS:
                        widen(q + 2)

            batches(pe, step)
            respond(B - 1)
            for q in range(CHUNKS):
                shrink(B - 1, q)


_INS = ['x', 'L0_conv_k_td', 'L0_conv_k_dt', 'L0_conv_k_lr', 'L0_conv_k_rl', 'L1_conv_w_fc1', 'L1_conv_ln1_w',
        'L1_conv_ln1_b', 'L1_conv_w_fc2', 'L1_conv_ln2_w', 'L1_conv_ln2_b', 'L1_conv_w_expand',
        'L1_conv_w_shrink', 'L1_conv_grn_gamma', 'L1_conv_grn_beta']
_OUT = ((8, 64, 64, 64), 'float32')


def kernel(**inputs):
    import numpy as _np
    import concourse.bacc as _bacc
    from concourse import mybir as _mybir
    from concourse.bass_utils import run_bass_kernel_spmd as _run

    nc = _bacc.Bacc("TRN2", target_bir_lowering=False, num_devices=1)
    arrays, args = {}, []
    for name in _INS:
        a = _np.ascontiguousarray(inputs[name])
        arrays[f"in_{name}_dram"] = a
        args.append(nc.dram_tensor(f"in_{name}_dram", a.shape, _mybir.dt.from_np(a.dtype), kind="ExternalInput").ap())
    shape, dtype = _OUT
    args.append(nc.dram_tensor("out_0_dram", shape, _mybir.dt.from_np(_np.dtype(dtype)), kind="ExternalOutput").ap())
    build(nc, *args)
    r = _run(nc, [arrays], core_ids=[0])
    return r.results[0]["out_0_dram"]
```
